# Optimizing a Trainium2 kernel written in Bass

```python
import numpy as np
import jax
import jax.numpy as jnp

def _softmax(x, axis=-1):
    return jax.nn.softmax(x, axis=axis)

def _gelu(x):
    return jax.nn.gelu(x, approximate=True)

def _silu(x):
    return jax.nn.silu(x)

def _sigmoid(x):
    return jax.nn.sigmoid(x)

def _layernorm(x, axis=-1, eps=1e-05):
    m = jnp.mean(x, axis=axis, keepdims=True)
    v = jnp.var(x, axis=axis, keepdims=True)
    return (x - m) / jnp.sqrt(v + eps)

def _scatter_add(tgt, idx, src, axis=0):
    return tgt.at[idx].add(src)

def _segment_sum(src, seg, n):
    return jax.ops.segment_sum(src, seg, n)
kernel_name = 'mk_gnn_preln_d2_gnn_r8_3a7a0c'

def setup_inputs(seed: int=0):
    np.random.seed(seed)
    _w = jnp.asarray

    def _rec_inputs():
        import jax
        import jax.numpy as jnp
        _gk = jax.random.key(seed)
        x = -0.0002117 + 1 * jax.random.normal(jax.random.fold_in(_gk, 1), (6250, 512), jnp.float32)
        src = jax.random.randint(jax.random.fold_in(_gk, 2), (100000,), 0, 6250, jnp.int32)
        dst = jnp.minimum((6250 * jax.random.uniform(jax.random.fold_in(_gk, 3), (100000,)) ** 2.0).astype(jnp.int32), 49999)
        _o = jnp.argsort(dst, stable=True)
        src = src[_o]
        dst = dst[_o]
        edge_attr_4 = 0.00171547 + 0.999346 * jax.random.normal(jax.random.fold_in(_gk, 12), (100000, 4), jnp.float32)
        edge_attr_8 = 0.000126197 + 0.999763 * jax.random.normal(jax.random.fold_in(_gk, 13), (100000, 8), jnp.float32)
        return (x, src, dst, edge_attr_4, edge_attr_8)
    x, src, dst, edge_attr_4, edge_attr_8 = _rec_inputs()

    def _L0_gnn_setup():
        import jax, jax.numpy as jnp
        import numpy as np
        N = 6250
        E = 50000
        D_IN = 512
        D_OUT = 512
        LN_EPS = 1e-05
        key = jax.random.key(seed)
        ks = jax.random.split(key, 8)
        x = jax.random.normal(ks[0], (N, D_IN), dtype=jnp.float32)
        src = jax.random.randint(ks[1], (E,), 0, N, dtype=jnp.int32)
        dst = jnp.sort(jax.random.randint(ks[2], (E,), 0, N, dtype=jnp.int32))
        bound = 1.0 / np.sqrt(D_IN)
        W_self = jax.random.uniform(ks[3], (D_IN, D_OUT), minval=-bound, maxval=bound, dtype=jnp.float32)
        b_self = jax.random.uniform(ks[4], (D_OUT,), minval=-bound, maxval=bound, dtype=jnp.float32)
        W_neigh = jax.random.uniform(ks[5], (D_IN, D_OUT), minval=-bound, maxval=bound, dtype=jnp.float32)
        gamma = jnp.ones((D_OUT,), dtype=jnp.float32)
        beta = jnp.zeros((D_OUT,), dtype=jnp.float32)
        alpha = jnp.array(0.25, dtype=jnp.float32)
        return {'x': x, 'src': src, 'dst': dst, 'W_self': W_self, 'b_self': b_self, 'W_neigh': W_neigh, 'gamma': gamma, 'beta': beta, 'alpha': alpha}
    _L0_gnn_all = _L0_gnn_setup()
    _L0_gnn_in = {k: v for k, v in _L0_gnn_all.items() if k in ('W_self', 'b_self', 'W_neigh', 'gamma', 'beta', 'alpha')}
    del _L0_gnn_all

    def _L1_gnn_setup():
        import jax, jax.numpy as jnp
        import numpy as np
        MUL = 128
        N_NODES = 1250
        N_EDGES = 20000
        R_BASIS = 8
        HIDDEN = 64
        W_NUMEL = 4 * MUL
        SQRT3 = 3.0 ** 0.5
        SILU_2MOM = 1.679177
        AVG_NUM_NEIGHBORS = 10.0

        def _lin_irreps(x0, x1, W0, W1):
            y0 = x0 @ W0 / jnp.sqrt(jnp.float32(W0.shape[0]))
            y1 = jnp.einsum('num,uv->nvm', x1, W1) / jnp.sqrt(jnp.float32(W1.shape[0]))
            return (y0, y1)

        def _forward(node_feats, edge_attrs, edge_feats, edge_index, W_up0, W_up1, W_mlp1, W_mlp2, W_mlp3, W_mlp4, W_out0, W_out1):
            num_nodes = node_feats.shape[0]
            sender, receiver = (edge_index[0], edge_index[1])
            x0 = node_feats[:, :MUL]
            x1 = node_feats[:, MUL:].reshape(num_nodes, MUL, 3)
            x0, x1 = _lin_irreps(x0, x1, W_up0, W_up1)
            h = edge_feats
            for W in (W_mlp1, W_mlp2, W_mlp3):
                h = SILU_2MOM * jax.nn.silu(h @ W / jnp.sqrt(jnp.float32(W.shape[0])))
            tpw = h @ W_mlp4 / jnp.sqrt(jnp.float32(W_mlp4.shape[0]))
            w1, w2, w3, w4 = jnp.split(tpw, 4, axis=-1)
            s0 = x0[sender]
            s1 = x1[sender]
            y0 = edge_attrs[:, 0:1]
            y1 = edge_attrs[:, 1:4]
            p1 = w1 * s0 * y0
            p2 = (w2 * s0)[:, :, None] * y1[:, None, :]
            p3 = w3[:, :, None] * s1 * y0[:, None, :]
            p4 = w4 * jnp.einsum('eum,em->eu', s1, y1) / SQRT3
            m0 = jnp.concatenate([p1, p4], axis=-1)
            m1 = jnp.concatenate([p2, p3], axis=1)
            msg0 = jax.ops.segment_sum(m0, receiver, num_segments=num_nodes)
            msg1 = jax.ops.segment_sum(m1, receiver, num_segments=num_nodes)
            o0, o1 = _lin_irreps(msg0, msg1, W_out0, W_out1)
            out = jnp.concatenate([o0, o1.reshape(num_nodes, 3 * MUL)], axis=-1)
            return out / AVG_NUM_NEIGHBORS
        key = jax.random.key(seed)
        ks = jax.random.split(key, 12)
        rn = lambda k, s: jax.random.normal(k, s, dtype=jnp.float32)
        return {'node_feats': rn(ks[0], (N_NODES, 4 * MUL)), 'edge_attrs': rn(ks[1], (N_EDGES, 4)), 'edge_feats': rn(ks[2], (N_EDGES, R_BASIS)), 'edge_index': jax.random.randint(ks[3], (2, N_EDGES), 0, N_NODES), 'W_up0': rn(ks[4], (MUL, MUL)), 'W_up1': rn(ks[5], (MUL, MUL)), 'W_mlp1': rn(ks[6], (R_BASIS, HIDDEN)), 'W_mlp2': rn(ks[7], (HIDDEN, HIDDEN)), 'W_mlp3': rn(ks[8], (HIDDEN, HIDDEN)), 'W_mlp4': rn(ks[9], (HIDDEN, W_NUMEL)), 'W_out0': rn(ks[10], (2 * MUL, MUL)), 'W_out1': rn(ks[11], (2 * MUL, MUL))}
    _L1_gnn_all = _L1_gnn_setup()
    _L1_gnn_in = {k: v for k, v in _L1_gnn_all.items() if k in ('W_up0', 'W_up1', 'W_mlp1', 'W_mlp2', 'W_mlp3', 'W_mlp4', 'W_out0', 'W_out1')}
    del _L1_gnn_all
    return {'x': x, 'src': src, 'dst': dst, 'edge_attr_4': edge_attr_4, 'edge_attr_8': edge_attr_8, 'L0_gnn_W_self': _L0_gnn_in['W_self'], 'L0_gnn_b_self': _L0_gnn_in['b_self'], 'L0_gnn_W_neigh': _L0_gnn_in['W_neigh'], 'L0_gnn_gamma': _L0_gnn_in['gamma'], 'L0_gnn_beta': _L0_gnn_in['beta'], 'L0_gnn_alpha': _L0_gnn_in['alpha'], 'L1_gnn_W_up0': _L1_gnn_in['W_up0'], 'L1_gnn_W_up1': _L1_gnn_in['W_up1'], 'L1_gnn_W_mlp1': _L1_gnn_in['W_mlp1'], 'L1_gnn_W_mlp2': _L1_gnn_in['W_mlp2'], 'L1_gnn_W_mlp3': _L1_gnn_in['W_mlp3'], 'L1_gnn_W_mlp4': _L1_gnn_in['W_mlp4'], 'L1_gnn_W_out0': _L1_gnn_in['W_out0'], 'L1_gnn_W_out1': _L1_gnn_in['W_out1']}

def reference(x, src, dst, edge_attr_4, edge_attr_8, L0_gnn_W_self, L0_gnn_b_self, L0_gnn_W_neigh, L0_gnn_gamma, L0_gnn_beta, L0_gnn_alpha, L1_gnn_W_up0, L1_gnn_W_up1, L1_gnn_W_mlp1, L1_gnn_W_mlp2, L1_gnn_W_mlp3, L1_gnn_W_mlp4, L1_gnn_W_out0, L1_gnn_W_out1):
    import jax
    import jax.numpy as jnp

    def _L0_gnn_ref(x, src, dst, W_self, b_self, W_neigh, gamma, beta, alpha):
        import jax, jax.numpy as jnp
        import numpy as np
        N = 6250
        E = 50000
        D_IN = 512
        D_OUT = 512
        LN_EPS = 1e-05
        deg = jax.ops.segment_sum(jnp.ones_like(src, dtype=x.dtype), dst, num_segments=N)
        inv_deg = 1.0 / jnp.maximum(deg, 1.0)
        agg = jax.ops.segment_sum(x[src], dst, num_segments=N)
        neigh = agg * inv_deg[:, None]
        h = x @ W_self + b_self + neigh @ W_neigh
        mu = jnp.mean(h, axis=-1, keepdims=True)
        var = jnp.mean(jnp.square(h - mu), axis=-1, keepdims=True)
        h = (h - mu) * jax.lax.rsqrt(var + LN_EPS) * gamma + beta
        h = jnp.where(h >= 0, h, alpha * h)
        return h + x

    def _L1_gnn_ref(node_feats, edge_attrs, edge_feats, edge_index, W_up0, W_up1, W_mlp1, W_mlp2, W_mlp3, W_mlp4, W_out0, W_out1):
        import jax, jax.numpy as jnp
        import numpy as np
        MUL = 128
        N_NODES = 1250
        N_EDGES = 20000
        R_BASIS = 8
        HIDDEN = 64
        W_NUMEL = 4 * MUL
        SQRT3 = 3.0 ** 0.5
        SILU_2MOM = 1.679177
        AVG_NUM_NEIGHBORS = 10.0

        def _lin_irreps(x0, x1, W0, W1):
            y0 = x0 @ W0 / jnp.sqrt(jnp.float32(W0.shape[0]))
            y1 = jnp.einsum('num,uv->nvm', x1, W1) / jnp.sqrt(jnp.float32(W1.shape[0]))
            return (y0, y1)

        def _forward(node_feats, edge_attrs, edge_feats, edge_index, W_up0, W_up1, W_mlp1, W_mlp2, W_mlp3, W_mlp4, W_out0, W_out1):
            num_nodes = node_feats.shape[0]
            sender, receiver = (edge_index[0], edge_index[1])
            x0 = node_feats[:, :MUL]
            x1 = node_feats[:, MUL:].reshape(num_nodes, MUL, 3)
            x0, x1 = _lin_irreps(x0, x1, W_up0, W_up1)
            h = edge_feats
            for W in (W_mlp1, W_mlp2, W_mlp3):
                h = SILU_2MOM * jax.nn.silu(h @ W / jnp.sqrt(jnp.float32(W.shape[0])))
            tpw = h @ W_mlp4 / jnp.sqrt(jnp.float32(W_mlp4.shape[0]))
            w1, w2, w3, w4 = jnp.split(tpw, 4, axis=-1)
            s0 = x0[sender]
            s1 = x1[sender]
            y0 = edge_attrs[:, 0:1]
            y1 = edge_attrs[:, 1:4]
            p1 = w1 * s0 * y0
            p2 = (w2 * s0)[:, :, None] * y1[:, None, :]
            p3 = w3[:, :, None] * s1 * y0[:, None, :]
            p4 = w4 * jnp.einsum('eum,em->eu', s1, y1) / SQRT3
            m0 = jnp.concatenate([p1, p4], axis=-1)
            m1 = jnp.concatenate([p2, p3], axis=1)
            msg0 = jax.ops.segment_sum(m0, receiver, num_segments=num_nodes)
            msg1 = jax.ops.segment_sum(m1, receiver, num_segments=num_nodes)
            o0, o1 = _lin_irreps(msg0, msg1, W_out0, W_out1)
            out = jnp.concatenate([o0, o1.reshape(num_nodes, 3 * MUL)], axis=-1)
            return out / AVG_NUM_NEIGHBORS
        return _forward(node_feats, edge_attrs, edge_feats, edge_index, W_up0, W_up1, W_mlp1, W_mlp2, W_mlp3, W_mlp4, W_out0, W_out1)
    edge_index = jnp.stack([src, dst])
    h = jnp.maximum(_layernorm(x, axis=-1), 0.0)
    x = x + _L0_gnn_ref(h, src, dst, L0_gnn_W_self, L0_gnn_b_self, L0_gnn_W_neigh, L0_gnn_gamma, L0_gnn_beta, L0_gnn_alpha)
    h = jnp.maximum(_layernorm(x, axis=-1), 0.0)
    x = x + _L1_gnn_ref(h, edge_attr_4, edge_attr_8, edge_index, L1_gnn_W_up0, L1_gnn_W_up1, L1_gnn_W_mlp1, L1_gnn_W_mlp2, L1_gnn_W_mlp3, L1_gnn_W_mlp4, L1_gnn_W_out0, L1_gnn_W_out1)
    return x

_drawn_inputs = setup_inputs


def setup_inputs(seed=0):
    import zlib

    import numpy as np

    out = dict(_drawn_inputs(seed))
    spreads = {'L0_gnn_gamma': (1.0, 0.2), 'L0_gnn_beta': (0.0, 0.1)}
    factors = {'L0_gnn_b_self': 2.674}
    for name, (base, spread) in spreads.items():
        noise = np.random.default_rng([zlib.crc32(name.encode()), seed]).standard_normal(out[name].shape)
        drawn = base * np.exp(spread * noise) if base else spread * noise
        out[name] = jnp.asarray(drawn.astype(out[name].dtype))
    for name, factor in factors.items():
        out[name] = (out[name] * factor).astype(out[name].dtype)
    return out
```

```python
import math
from contextlib import ExitStack

import numpy as np
import concourse.bass as bass
from concourse import mybir

F32 = mybir.dt.float32
I32 = mybir.dt.int32
ALU = mybir.AluOpType
ACT = mybir.ActivationFunctionType
AX = mybir.AxisListType

P = 128
N_NODES, D = 6250, 512
N_EDGES = 100000
KC = D // P
NT = -(-N_NODES // P)
NP = NT * P
WINDOW_ROWS = NP + P
TJ = 4
GE = TJ * P
NG = -(-N_EDGES // GE)
MUL = 128
HID = 64
BASIS = 8
HALF = GE // 2
LN_EPS = 1e-5
SILU_2MOM = 1.679177
AVG_NEIGHBORS = 10.0
AW = D + 1
B_SLOTS, B_LAG = 4, 3
D_SLOTS, D_LAG = 2, 2
DEAD = -1.0e6
assert NG % B_SLOTS == 0 and NG % D_SLOTS == 0 and NG % 2 == 0 and NT % 2 == 1
GP = NG // 2


def gnn_kernel(nc, x, src_g, dst_rows, dst_cols, attr_cols, feat_g, w_self, w_neigh, b_self, gamma, beta,
               alpha, w_up0, w_up1, w_mlp1, w_mlp2, w_mlp3, w_mlp4, w_out0, w_out1, out):
    table0 = nc.dram_tensor("table0", (NP, D), F32, kind="Internal").ap()
    table1 = nc.dram_tensor("table1", (NP, D), F32, kind="Internal").ap()
    resid = nc.dram_tensor("resid", (NP, D), F32, kind="Internal").ap()
    acc0 = nc.dram_tensor("acc0", (WINDOW_ROWS, AW), F32, kind="Internal").ap()
    meta = nc.dram_tensor("meta", (2, NG), I32, kind="Internal").ap()

    with ExitStack() as ctx:
        def sb(name, shape, dt=F32):
            return ctx.enter_context(nc.sbuf_tensor(name, shape, dt))

        def sem(name):
            return ctx.enter_context(nc.semaphore(name))

        def carve(arena, sizes):
            views, at = [], 0
            for shape in sizes:
                n = math.prod(shape)
                v = arena[:, at:at + n]
                if len(shape) == 2:
                    v = v.rearrange("p (a b) -> p a b", a=shape[0])
                if len(shape) == 3:
                    v = v.rearrange("p (a b c) -> p a b c", a=shape[0], b=shape[1])
                views.append(v)
                at += n
            assert at <= arena.shape[1], (at, arena.shape)
            return views

        big = sb("big", [P, NT * D])
        work = sb("work", [P, B_SLOTS * (TJ * D + TJ * P) + 2 * AW + 64])
        self_part = big
        bias_bc, gamma_bc, beta_bc = sb("bias_bc", [P, D]), sb("gamma_bc", [P, D]), sb("beta_bc", [P, D])
        alpha_bc = sb("alpha_bc", [P, 1])
        eps_t = sb("eps_t", [P, 1])
        ident = sb("ident", [P, P])
        iota_n = sb("iota_n", [P, P])
        window_start = sb("window_start", [P, NT])
        ones = sb("ones", [P, 2])
        rel = sb("rel", [P, NG * TJ])
        rel_w = sb("rel_w", [P, TJ])
        src_idx = [sb(f"src_idx{s}", [P, TJ], I32) for s in range(B_SLOTS)]
        meta_row = sb("meta_row", [1, 4 * NG], I32)
        START, MORE, BEFORE = 0, NG, 2 * NG
        stats = sb("stats", [P, 2, 6])
        mean_var = sb("mean_var", [P, 2, 2])
        std = sb("std", [P, 2, 1])
        rstd = sb("rstd", [P, 2, 1])
        shift = sb("shift", [P, 2, 1])
        stats2 = sb("stats2", [P, 2, 6])
        mean_var2 = sb("mean_var2", [P, 2, 2])
        std2 = sb("std2", [P, 2, 1])
        rstd2 = sb("rstd2", [P, 2, 1])
        shift2 = sb("shift2", [P, 2, 1])
        deg = sb("deg", [P, 2, 1])
        rdeg = sb("rdeg", [P, 2, 1])
        w_up = sb("w_up", [P, 2, MUL])

        wn_sb, ws_sb, xt, ht, h_t, hn_t, res_t = carve(
            work, [(KC, D), (KC, D), (2, D), (2, D), (2, D), (2, D), (2, D)])
        rows_b, sel_b, stage_b = carve(work, [(B_SLOTS, TJ * D), (B_SLOTS, TJ * P), (2, AW)])
        acc_t, res_c, h0_t, y_t, neg_t, x2_t, h2_t, h2T_t, up_t = carve(
            work, [(2, AW), (2, D), (2, D), (2, D), (1, D), (2, D), (2, D), (1, D), (2, D)])
        (rows_d, sel_d, msg, q_t, feat_t, h1, h2, h3, sum_sb, sumT_sb, o_sb, attr, w1_sb, w2_sb, w3_sb, w4_sb,
         wout_sb) = carve(
            big, [(D_SLOTS, TJ * D), (D_SLOTS, TJ * P), (2, 8 * MUL), (2, 3 * MUL), (D_SLOTS, HALF),
                  (1, HALF), (1, HALF), (2, HALF), (1, 8 * MUL), (1, 8 * MUL), (2, 4 * MUL),
                  (1, NG * TJ * 4), (1, P), (1, P), (1, P), (1, D), (4, MUL)])
        dst_r_i = sb("dst_r_i", [GP, 2 * GE], I32)
        dst_c_i = sb("dst_c_i", [P, NG * TJ], I32)
        least = sb("least", [GP, 2], I32)
        more = sb("more", [GP, 2], I32)
        start_bc = sb("start_bc", [P, NG], I32)
        more_f = sb("more_f", [1, NG])
        zero_f = sb("zero_f", [1, NG])
        prefix_f = sb("prefix_f", [1, NG])

        psum = ctx.enter_context(nc.psum_tensor("psum", [P, 8, D], F32))
        flat = psum[:, :, :].rearrange("p b n -> p (b n)")

        s_bar = sem("s_barrier")
        s_held = sem("s_waits_held")
        s_w = sem("s_weights_in")
        s_dst = sem("s_dst_in")
        s_const = sem("s_constants_made")
        s_pool_const = sem("s_pool_constants")
        s_meta_made = sem("s_meta_made")
        s_meta_out = sem("s_meta_out")
        s_meta_in = sem("s_meta_in")
        s_setup = sem("s_setup_chain")
        s_zero = sem("s_zero_rows")
        s_zeroed = sem("s_zero_tile")

        ENGINES = 5

        def barrier(eng, n):
            eng.drain().then_inc(s_bar, 1)
            eng.wait_ge(s_bar, ENGINES * n)

        def hold(eng):
            eng.sem_inc(s_held, 1)

        class Chain:
            def __init__(self, eng, s, base=0):
                self.eng, self.s, self.base, self.n = eng, s, base, 0

            def link(self, ins):
                self.n += 1
                ins.then_inc(self.s, 1)
                self.eng.wait_ge(self.s, self.base + self.n)

        def pair(r, s):
            return r * 2 + s

        a_x_in = [sem(f"a_x_in{s}") for s in range(2)]
        a_chain = sem("a_vector_chain")
        a_var = sem("a_variance")
        a_std = sem("a_std")
        a_shift = sem("a_shift")
        a_h = sem("a_h_ready")
        a_T = sem("a_h_transposed")
        a_Tc = sem("a_h_transposed_copied")
        a_mm = sem("a_products")
        a_hn = sem("a_neigh_copied")
        a_self = sem("a_self_kept")
        a_res = sem("a_resid_made")
        a_res_out = sem("a_resid_out")
        a_hn_out = sem("a_table_out")
        a_out_free = sem("a_stored")

        class EdgeSemsB:
            def __init__(self, name, slots):
                self.slots = slots
                self.idx_in = [sem(f"{name}_idx_in{s}") for s in range(slots)]
                self.rows_in = [sem(f"{name}_rows_in{s}") for s in range(slots)]
                self.sel = sem(f"{name}_selection_made")
                self.relw = sem(f"{name}_rel_window")
                self.bufs = min(2, slots)
                self.summed = sem(f"{name}_summed")
                self.staged = sem(f"{name}_staged")
                self.stage_free = sem(f"{name}_stage_free")
                self.added = sem(f"{name}_added")

        bm = EdgeSemsB("b", B_SLOTS)
        bx = EdgeSemsB("bx", 1)

        c_in = [sem(f"c_in{s}") for s in range(2)]
        c_chain = sem("c_vector_chain")
        c_var, c_std, c_shift, c_y = sem("c_var"), sem("c_std"), sem("c_shift"), sem("c_y")
        c_var2, c_std2, c_shift2 = sem("c_var2"), sem("c_std2"), sem("c_shift2")
        c_x2 = sem("c_x2_made")
        c_h2 = sem("c_h2_made")
        c_T, c_Tc, c_up = sem("c_h2_transposed"), sem("c_h2_transposed_copied"), sem("c_up_products")
        c_upc = sem("c_up_copied")
        c_x2_out, c_up_out = sem("c_x2_out"), sem("c_table_out")
        c_out_free = sem("c_stored")

        class EdgeSemsD:
            def __init__(self, name, slots):
                self.slots = self.bufs = slots
                self.feat_in = [sem(f"{name}_feat_in{s}") for s in range(slots)]
                self.idx_in = [sem(f"{name}_idx_in{s}") for s in range(slots)]
                self.rows_in = [sem(f"{name}_rows_in{s}") for s in range(slots)]
                self.relw = sem(f"{name}_rel_window")
                self.sel = sem(f"{name}_selection_made")
                self.layer = [sem(f"{name}_layer{n}") for n in range(3)]
                self.act = [sem(f"{name}_layer{n}_silu") for n in range(3)]
                self.weights = sem(f"{name}_edge_weights")
                self.q = sem(f"{name}_q_chain")
                self.msg = sem(f"{name}_messages")
                self.tile = sem(f"{name}_tile_summed")
                self.sum_copied = sem(f"{name}_sum_copied")
                self.T = sem(f"{name}_sum_transposed")
                self.T_copied = sem(f"{name}_sum_transposed_copied")
                self.o = sem(f"{name}_output_maps")
                self.staged = sem(f"{name}_staged")
                self.stage_free = sem(f"{name}_stage_free")
                self.added = sem(f"{name}_added")

        dm = EdgeSemsD("d", D_SLOTS)
        dx = EdgeSemsD("dx", 1)
        s_dw = sem("d_weights_in")
        s_dw_scaled = sem("d_weights_scaled")

        def general_pass(eng, x, step):
            any_more = eng.value_load(meta_row[0:1, 3 * NG:3 * NG + 1], min_val=0, max_val=NG * NT)
            with eng.If(any_more > 0):
                with eng.Fori(0, NG) as g:
                    n_more = eng.value_load(meta_row[0:1, bass.ds(g + MORE, 1)], min_val=0, max_val=NT - 1)
                    before = eng.value_load(meta_row[0:1, bass.ds(g + BEFORE, 1)], min_val=0, max_val=NG * NT)
                    with eng.If(n_more > 0):
                        with eng.Fori(0, n_more) as w:
                            step(x, g, w + 1, before + w)
                    eng.nop()
            eng.nop()

        block = ctx.enter_context(nc.Block())

        @block.sync
        def _(sp):
            sp.dma_start(dst_r_i[:, :], dst_rows).then_inc(s_dst, 16)
            sp.dma_start(dst_c_i[:, :], dst_cols).then_inc(s_dst, 16)
            sp.dma_start(wn_sb, w_neigh.rearrange("(c p) n -> p c n", p=P)).then_inc(s_w, 16)
            sp.dma_start(ws_sb, w_self.rearrange("(c p) n -> p c n", p=P)).then_inc(s_w, 16)
            sp.dma_start(bias_bc[:, :], b_self).then_inc(s_w, 16)
            sp.dma_start(gamma_bc[:, :], gamma).then_inc(s_w, 16)
            sp.dma_start(beta_bc[:, :], beta).then_inc(s_w, 16)
            sp.dma_start(alpha_bc[:, :], alpha).then_inc(s_w, 16)
            sp.dma_start(w_up[:, 0, :], w_up0).then_inc(s_w, 16)
            sp.dma_start(w_up[:, 1, :], w_up1).then_inc(s_w, 16)

            def load_x(i, s):
                t = pair(i, s)
                sp.wait_ge(a_res, t + 1)
                sp.dma_start(xt[:, s, :], x[bass.ds(t * P, P), :]).then_inc(a_x_in[s], 16)

            sp.wait_ge(s_meta_made, 1)
            sp.dma_start(meta[0, :].rearrange("(p c) -> p c", c=2), least[:, :]).then_inc(s_meta_out, 16)
            sp.dma_start(meta[1, :].rearrange("(p c) -> p c", c=2), more[:, :]).then_inc(s_meta_out, 16)
            sp.wait_ge(s_meta_out, 32)
            sp.dma_start(meta_row[0:1, 0:2 * NG], meta.rearrange("(a r) g -> a (r g)", a=1)).then_inc(s_meta_in, 16)
            sp.dma_start(start_bc[:, :], meta[0, :].partition_broadcast(P)).then_inc(s_meta_in, 16)

            with sp.Fori(0, NT // 2) as i:
                for s in range(2):
                    load_x(i, s)
            load_x(NT // 2, 0)
            sp.wait_ge(s_zeroed, 1)
            barrier(sp, 1)

            def idx_b(x_, g, i, s, k):
                sp.wait_ge(x_.summed, k + 1)
                sp.dma_start(src_idx[s][:, :], src_g[bass.ds(g, 1), :, :].rearrange("a p j -> (a p) j")
                             ).then_inc(x_.idx_in[s], 16)

            with sp.Fori(0, NG // B_SLOTS) as i:
                for s in range(B_SLOTS):
                    k = i * B_SLOTS + s
                    idx_b(bm, k, i, s, k)
            barrier(sp, 2)
            general_pass(sp, bx, lambda x_, g, w, k: idx_b(x_, g, k, 0, k))
            barrier(sp, 3)

            def load_c(i, s):
                t = pair(i, s)
                sp.wait_ge(c_x2, t + 1)
                sp.dma_start(acc_t[:, s, :], acc0[bass.ds(t * P, P), :]).then_inc(c_in[s], 16)
                sp.dma_start(res_c[:, s, :], resid[bass.ds(t * P, P), :]).then_inc(c_in[s], 16)

            with sp.Fori(0, NT // 2) as i:
                for s in range(2):
                    load_c(i, s)
            load_c(NT // 2, 0)
            barrier(sp, 4)

            sp.dma_start(attr[:, 0, :], attr_cols).then_inc(s_dw, 16)
            sp.dma_start(w1_sb[0:2 * BASIS, 0, :], w_mlp1).then_inc(s_dw, 16)
            sp.dma_start(w2_sb[:, 0, :], w_mlp2).then_inc(s_dw, 16)
            sp.dma_start(w3_sb[:, 0, :], w_mlp3).then_inc(s_dw, 16)
            sp.dma_start(w4_sb[:, 0, :], w_mlp4).then_inc(s_dw, 16)
            sp.dma_start(wout_sb[:, 0:2, :], w_out0.rearrange("(c p) n -> p c n", p=P)).then_inc(s_dw, 16)
            sp.dma_start(wout_sb[:, 2:4, :], w_out1.rearrange("(c p) n -> p c n", p=P)).then_inc(s_dw, 16)

            def inputs_d(x_, g, s, k):
                sp.wait_ge(x_.msg, (k + 1) * TJ)
                sp.dma_start(src_idx[s][:, :], src_g[bass.ds(g, 1), :, :].rearrange("a p j -> (a p) j")
                             ).then_inc(x_.idx_in[s], 16)
                sp.dma_start(feat_t[0:2 * BASIS, s, :], feat_g[bass.ds(g, 1), :, :].rearrange("a f e -> (a f) e")
                             ).then_inc(x_.feat_in[s], 16)

            with sp.Fori(0, NG // D_SLOTS) as i:
                for s in range(D_SLOTS):
                    k = i * D_SLOTS + s
                    inputs_d(dm, k, s, k)
            barrier(sp, 5)
            general_pass(sp, dx, lambda x_, g, w, k: inputs_d(x_, g, 0, k))

        @block.gpsimd
        def _(pool):
            nc.gpsimd.memset(ident[:, :], 0.0).then_inc(s_pool_const, 1)
            nc.gpsimd.memset(ones[:, :], 1.0)
            nc.gpsimd.memset(eps_t[:, :], LN_EPS)
            nc.gpsimd.iota(iota_n[:, :], pattern=[[1, P]], base=0, channel_multiplier=0,
                           allow_small_or_imprecise_dtypes=True)
            nc.gpsimd.iota(window_start[:, :], pattern=[[P, NT]], base=0, channel_multiplier=0,
                           allow_small_or_imprecise_dtypes=True)
            pool.wait_ge(s_pool_const, 1)
            nc.gpsimd.affine_select(out=ident[:, :], in_=ident[:, :], compare_op=ALU.not_equal, fill=1.0,
                                    base=0, pattern=[[-1, P]], channel_multiplier=1).then_inc(s_const, 1)

            pool.wait_ge(s_zeroed, 1)
            with pool.Fori(0, WINDOW_ROWS // P) as t:
                pool.dma_start(acc0[bass.ds(t * P, P), :], big[:, 0:AW]).then_inc(s_zero, 16)
            pool.dma_start(out[NP:WINDOW_ROWS, :], big[:, 0:D]).then_inc(s_zero, 16)
            pool.wait_ge(s_zero, 16 * (WINDOW_ROWS // P + 1))

            pool.sem_inc(a_out_free, 2)

            def store_a(i, s):
                t = pair(i, s)
                pool.wait_ge(a_res, t + 3)
                hold(pool)
                pool.dma_start(resid[bass.ds(t * P, P), :], res_t[:, s, :]).then_inc(a_res_out, 16)
                pool.wait_ge(a_hn, t + 3)
                hold(pool)
                pool.dma_start(table0[bass.ds(t * P, P), :], hn_t[:, s, :]).then_inc(a_hn_out, 16)
                pool.wait_ge(a_res_out, t * 16 + 16)
                pool.wait_ge(a_hn_out, t * 16 + 16)
                pool.sem_inc(a_out_free, 1)

            with pool.Fori(0, NT // 2) as i:
                for s in range(2):
                    store_a(i, s)
            store_a(NT // 2, 0)
            barrier(pool, 1)

            def gather(x_, table, rows, i, s, k, rows_free, per_step):
                pool.wait_ge(x_.idx_in[s], (i + 1) * 16)
                pool.wait_ge(rows_free, (k + 1) * per_step)
                hold(pool)
                for j in range(TJ):
                    nc.gpsimd.indirect_dma_start(
                        rows[:, s, j * D:(j + 1) * D], None, table,
                        bass.IndirectOffsetOnAxis(ap=src_idx[s][:, j:j + 1], axis=0)).then_inc(x_.rows_in[s], 16)

            def add_window(x_, target, stage, g, s, k, first=False):
                row = pool.value_load(meta_row[0:1, bass.ds(g + START, 1)], min_val=0, max_val=N_NODES - 1)
                pool.wait_ge(x_.staged, k + 1 + x_.bufs)
                if first:
                    hold(pool)
                else:
                    pool.wait_ge(x_.added, k * 16)
                    pool.sem_inc(x_.stage_free, 1)
                pool.dma_start(target[bass.ds(row, P), :], stage[:, s, :], accum_op=ALU.add
                               ).then_inc(x_.added, 16)

            def add_window_alone(x_, target, stage, g, w, k):
                row0 = pool.value_load(meta_row[0:1, bass.ds(g + START, 1)], min_val=0, max_val=N_NODES - 1)
                row = nc.s_assert_within(row0 + w * P, 0, WINDOW_ROWS - P)
                pool.wait_ge(x_.staged, k + 1 + x_.bufs)
                hold(pool)
                pool.dma_start(target[bass.ds(row, P), :], stage[:, 0, :], accum_op=ALU.add
                               ).then_inc(x_.added, 16)
                pool.wait_ge(x_.added, (k + 1) * 16)
                pool.sem_inc(x_.stage_free, 1)

            def pipelined(x_, table, rows, target, stage, lag, rows_free, per_step):
                slots = x_.slots

                def step(i, s):
                    k = i * slots + s
                    if not (isinstance(k, int) and k < lag):
                        add_window(x_, target, stage, k - lag, (s - lag) % 2, k - lag,
                                   first=isinstance(k, int) and k == lag)
                    gather(x_, table, rows, i, s, k, rows_free, per_step)

                first_i = -(-(lag + 1) // slots)
                for i in range(first_i):
                    for s in range(slots):
                        step(i, s)
                with pool.Fori(first_i, NG // slots) as i:
                    for s in range(slots):
                        step(i, s)
                for k in range(NG - lag, NG):
                    add_window(x_, target, stage, k, k % 2, k)
                pool.wait_ge(x_.added, NG * 16)

            pool.sem_inc(bm.stage_free, bm.bufs)
            pool.sem_inc(bx.stage_free, bx.bufs)
            pipelined(bm, table0, rows_b, acc0, stage_b, B_LAG, bm.summed, 1)
            barrier(pool, 2)

            def general_b(x_, g, w, k):
                gather(x_, table0, rows_b, k, 0, k, x_.summed, 1)
                add_window_alone(x_, acc0, stage_b, g, w, k)
            general_pass(pool, bx, general_b)
            barrier(pool, 3)

            pool.sem_inc(c_out_free, 2)

            def store_c(i, s):
                t = pair(i, s)
                pool.wait_ge(c_x2, t + 3)
                hold(pool)
                pool.dma_start(out[bass.ds(t * P, P), :], x2_t[:, s, :]).then_inc(c_x2_out, 16)
                pool.wait_ge(c_upc, t + 3)
                hold(pool)
                pool.dma_start(table1[bass.ds(t * P, P), :], up_t[:, s, :]).then_inc(c_up_out, 16)
                pool.wait_ge(c_x2_out, t * 16 + 16)
                pool.wait_ge(c_up_out, t * 16 + 16)
                pool.sem_inc(c_out_free, 1)

            with pool.Fori(0, NT // 2) as i:
                for s in range(2):
                    store_c(i, s)
            store_c(NT // 2, 0)
            barrier(pool, 4)

            pool.sem_inc(dm.stage_free, dm.bufs)
            pool.sem_inc(dx.stage_free, dx.bufs)
            pipelined(dm, table1, rows_d, out, o_sb, D_LAG, dm.msg, TJ)
            barrier(pool, 5)

            def general_d(x_, g, w, k):
                gather(x_, table1, rows_d, k, 0, k, x_.msg, TJ)
                add_window_alone(x_, out, o_sb, g, w, k)
            general_pass(pool, dx, general_d)

        @block.scalar
        def _(act):
            act.wait_ge(s_const, 1)
            act.sem_inc(a_hn, 2)

            def a_front(i, s):
                t = pair(i, s)
                act.wait_ge(a_var, t + 1)
                nc.scalar.activation(std[:, s, :], mean_var[:, s, 1:2], ACT.Sqrt, bias=eps_t[:, :]
                                     ).then_inc(a_std, 1)
                act.wait_ge(a_shift, t + 1)
                act.wait_ge(a_res, t + 1)
                nc.scalar.activation(ht[:, s, :], xt[:, s, :], ACT.Relu, bias=shift[:, s, :],
                                     scale=rstd[:, s, :]).then_inc(a_h, 1)

            def a_back(i, s):
                t = pair(i, s)
                act.wait_ge(a_T, t + 1)
                nc.scalar.activation(h_t[:, s, :], psum[:, s, :], ACT.Copy).then_inc(a_Tc, 1)
                act.wait_ge(a_mm, t + 1)
                act.wait_ge(a_out_free, t + 1)
                nc.scalar.activation(hn_t[:, s, :], psum[:, 2 + s, :], ACT.Copy).then_inc(a_hn, 1)

            a_front(0, 0)
            with act.Fori(0, NT // 2) as i:
                a_front(i, 1)
                a_back(i, 0)
                a_front(i + 1, 0)
                a_back(i, 1)
            a_back(NT // 2, 0)
            barrier(act, 1)

            act.sem_inc(bm.staged, bm.bufs)
            act.sem_inc(bx.staged, bx.bufs)

            def b_step(x_, s2, k):
                act.wait_ge(x_.summed, k + 1 + x_.slots)
                act.wait_ge(x_.stage_free, k + 1)
                nc.scalar.activation(stage_b[:, s2, :], flat[:, 2 * s2 * D:2 * s2 * D + AW], ACT.Copy
                                     ).then_inc(x_.staged, 1)

            with act.Fori(0, NG // 2) as i:
                for s in range(2):
                    b_step(bm, s, pair(i, s))
            barrier(act, 2)
            general_pass(act, bx, lambda x_, g, w, k: b_step(x_, 0, k))
            barrier(act, 3)

            act.sem_inc(c_h2, 2)
            act.sem_inc(c_upc, 2)

            def c_std1(i, s):
                act.wait_ge(c_var, pair(i, s) + 1)
                nc.scalar.activation(std[:, s, :], mean_var[:, s, 1:2], ACT.Sqrt, bias=eps_t[:, :]
                                     ).then_inc(c_std, 1)

            def c_norm1(i, s):
                act.wait_ge(c_shift, pair(i, s) + 1)
                nc.scalar.activation(y_t[:, s, :], h0_t[:, s, :], ACT.Identity, bias=shift[:, s, :],
                                     scale=rstd[:, s, :]).then_inc(c_y, 1)

            def c_norm2(i, s):
                act.wait_ge(c_var2, pair(i, s) + 1)
                nc.scalar.activation(std2[:, s, :], mean_var2[:, s, 1:2], ACT.Sqrt, bias=eps_t[:, :]
                                     ).then_inc(c_std2, 1)
                act.wait_ge(c_shift2, pair(i, s) + 1)
                nc.scalar.activation(h2_t[:, s, :], x2_t[:, s, :], ACT.Relu, bias=shift2[:, s, :],
                                     scale=rstd2[:, s, :]).then_inc(c_h2, 1)

            def c_copies(i, s):
                t = pair(i, s)
                act.wait_ge(c_T, t + 1)
                nc.scalar.activation(h2T_t[:, 0, :], psum[:, s, :], ACT.Copy).then_inc(c_Tc, 1)
                act.wait_ge(c_up, t + 1)
                act.wait_ge(c_out_free, t + 1)
                nc.scalar.activation(up_t[:, s, :], psum[:, 2 + s, :], ACT.Copy).then_inc(c_upc, 1)

            def c_both(i, s, i1, s1):
                c_std1(i1, s1)
                c_norm2(i, s)
                c_norm1(i1, s1)
                c_copies(i, s)

            c_std1(0, 0)
            c_norm1(0, 0)
            with act.Fori(0, NT // 2) as i:
                c_both(i, 0, i, 1)
                c_both(i, 1, i + 1, 0)
            c_norm2(NT // 2, 0)
            c_copies(NT // 2, 0)
            barrier(act, 4)

            act.sem_inc(dm.act[2], 1)
            act.sem_inc(dx.act[2], 1)
            act.sem_inc(dm.sum_copied, 1)
            act.sem_inc(dx.sum_copied, 1)
            act.sem_inc(dm.T_copied, 1)
            act.sem_inc(dx.T_copied, 1)
            act.sem_inc(dm.staged, dm.bufs)
            act.sem_inc(dx.staged, dx.bufs)
            scales = [BASIS ** -0.5, SILU_2MOM * HID ** -0.5, SILU_2MOM * HID ** -0.5]

            def silu(x_, n, k, s):
                act.wait_ge(x_.layer[n], k + 1)
                to = (h1[:, 0, :], h2[:, 0, :], h3[:, s, :])[n]
                nc.scalar.activation(to, psum[:, 0, 0:HALF], ACT.Silu, scale=scales[n]).then_inc(x_.act[n], 1)

            def copy_sum(x_, k):
                act.wait_ge(x_.tile, k * TJ + TJ + 2)
                act.wait_ge(x_.T, k + 1)
                nc.scalar.activation(sum_sb[:, 0, :], flat[:, 3 * D:5 * D], ACT.Copy).then_inc(x_.sum_copied, 1)

            def copy_T(x_, k):
                act.wait_ge(x_.T, k + 2)
                act.wait_ge(x_.o, k + 1)
                nc.scalar.activation(sumT_sb[:, 0, :], flat[:, 5 * D:7 * D], ACT.Copy).then_inc(x_.T_copied, 1)

            def copy_o(x_, k, s):
                act.wait_ge(x_.o, k + 2)
                act.wait_ge(x_.stage_free, k + 1)
                nc.scalar.activation(o_sb[:, s, 0:MUL], psum[:, 7, 0:MUL], ACT.Copy)
                nc.scalar.activation(o_sb[:, s, MUL:4 * MUL].rearrange("p (v m) -> p m v", m=3),
                                     psum[:, 7, MUL:4 * MUL].rearrange("p (m v) -> p m v", m=3),
                                     ACT.Copy).then_inc(x_.staged, 1)

            def d_step(k, s, first=False, last=False):
                if not first:
                    copy_sum(dm, k - 1)
                    copy_T(dm, k - 1)
                if not last:
                    silu(dm, 0, k + 1, 1 - s)
                    silu(dm, 1, k + 1, 1 - s)
                if not first:
                    copy_o(dm, k - 1, 1 - s)
                if not last:
                    silu(dm, 2, k + 1, 1 - s)

            for n in range(3):
                silu(dm, n, 0, 0)
            d_step(0, 0, first=True)
            d_step(1, 1)
            with act.Fori(1, NG // 2 - 1) as i:
                d_step(pair(i, 0), 0)
                d_step(pair(i, 1), 1)
            d_step(NG - 2, 0)
            d_step(NG - 1, 1, last=True)
            copy_sum(dm, NG - 1)
            copy_T(dm, NG - 1)
            copy_o(dm, NG - 1, 1)
            barrier(act, 5)

            def general_d(x_, g, w, k):
                for n in range(3):
                    silu(x_, n, k, 0)
                copy_sum(x_, k)
                copy_T(x_, k)
                copy_o(x_, k, 0)
            general_pass(act, dx, general_d)

        @block.vector
        def _(dve):
            setup = Chain(dve, s_setup)
            nc.vector.memset(big[:, 0:AW], 0.0).then_inc(s_zeroed, 1)
            dve.wait_ge(s_dst, 32)
            rows2 = dst_r_i[:, :].rearrange("p (c e) -> p c e", c=2)
            setup.link(nc.vector.tensor_reduce(least[:, :], rows2, AX.X, ALU.min))
            setup.link(nc.vector.tensor_reduce(more[:, :], rows2, AX.X, ALU.max))
            setup.link(nc.vector.tensor_tensor(more[:, :], more[:, :], least[:, :], ALU.subtract))
            nc.vector.tensor_scalar(more[:, :], more[:, :], int(math.log2(P)), None, ALU.arith_shift_right
                                    ).then_inc(s_meta_made, 1)
            dve.wait_ge(s_meta_in, 32)
            setup.link(nc.vector.memset(zero_f[:, :], 0.0))
            setup.link(nc.vector.tensor_copy(more_f[:, :], meta_row[0:1, MORE:MORE + NG]))
            setup.link(nc.vector.tensor_tensor_scan(prefix_f[:, :], more_f[:, :], zero_f[:, :], 0.0,
                                                    ALU.add, ALU.add))
            setup.link(nc.vector.tensor_copy(meta_row[0:1, 3 * NG:3 * NG + 1], prefix_f[0:1, NG - 1:NG]))
            setup.link(nc.vector.tensor_tensor(meta_row[0:1, BEFORE:BEFORE + NG], prefix_f[:, :], more_f[:, :],
                                               ALU.subtract))
            start_v = start_bc[:, :].unsqueeze(2).to_broadcast([P, NG, TJ])
            setup.link(nc.vector.tensor_tensor(rel[:, :].rearrange("p (g j) -> p g j", j=TJ),
                                               dst_c_i[:, :].rearrange("p (g j) -> p g j", j=TJ), start_v,
                                               ALU.subtract))
            full, part = divmod(N_EDGES, P)
            for p0 in range(part, P, 32):
                setup.link(nc.vector.memset(rel[p0:p0 + 32, full:full + 1], DEAD))
            setup.link(nc.vector.memset(rel[:, full + 1:], DEAD))
            dve.wait_ge(s_w, 8 * 16)
            setup.link(nc.vector.tensor_scalar(w_up[:, :, :], w_up[:, :, :], MUL ** -0.5, None, ALU.mult))
            dve.wait_ge(s_zero, 16 * (WINDOW_ROWS // P + 1))

            dve.sem_inc(a_res, 2)
            dve.sem_inc(a_self, 2)

            def a_front(i, s):
                t = pair(i, s)
                chain = Chain(dve, a_chain, t * 2)
                dve.wait_ge(a_x_in[s], (i + 1) * 16)
                chain.link(nc.vector.bn_stats(stats[:, s, :], xt[:, s, :]))
                hold(dve)
                nc.vector.bn_aggr(mean_var[:, s, :], stats[:, s, :]).then_inc(a_var, 1)
                dve.wait_ge(a_std, t + 1)
                chain.link(nc.vector.reciprocal(rstd[:, s, :], std[:, s, :]))
                nc.vector.tensor_scalar(shift[:, s, :], mean_var[:, s, 0:1], rstd[:, s, :], -1.0,
                                        ALU.mult, ALU.mult).then_inc(a_shift, 1)

            def a_back(i, s):
                t = pair(i, s)
                dve.wait_ge(a_h, t + 1)
                dve.wait_ge(a_out_free, t + 1)
                nc.vector.tensor_tensor(res_t[:, s, :], xt[:, s, :], ht[:, s, :], ALU.add).then_inc(a_res, 1)
                dve.wait_ge(a_mm, t + 1)
                nc.vector.tensor_tensor(self_part[:, bass.ds(t * D, D)], psum[:, 4 + s, :], bias_bc[:, :],
                                        ALU.add).then_inc(a_self, 1)

            a_front(0, 0)
            with dve.Fori(0, NT // 2) as i:
                a_front(i, 1)
                a_back(i, 0)
                a_front(i + 1, 0)
                a_back(i, 1)
            a_back(NT // 2, 0)
            barrier(dve, 1)

            def select(x_, sel, rel_at, s):
                for j in range(TJ):
                    last = nc.vector.tensor_scalar(sel[:, s, j * P:(j + 1) * P], iota_n[:, :], rel_at(j), None,
                                                   ALU.is_equal)
                last.then_inc(x_.sel, 1)

            def rel_main(g):
                return lambda j: rel[:, bass.ds(g * TJ + j, 1)]

            def rel_of_window(x_, g, w, k):
                nc.vector.tensor_scalar(rel_w[:, :], rel[:, bass.ds(g * TJ, TJ)], window_start[:, bass.ds(w, 1)],
                                        None, ALU.subtract).then_inc(x_.relw, 1)
                dve.wait_ge(x_.relw, k + 1)
                return lambda j: rel_w[:, j:j + 1]

            with dve.Fori(0, NG // B_SLOTS) as i:
                for s in range(B_SLOTS):
                    k = i * B_SLOTS + s
                    dve.wait_ge(bm.summed, k + 1)
                    select(bm, sel_b, rel_main(k), s)
            barrier(dve, 2)

            def general_b(x_, g, w, k):
                dve.wait_ge(x_.summed, k + 1)
                select(x_, sel_b, rel_of_window(x_, g, w, k), 0)
            general_pass(dve, bx, general_b)
            barrier(dve, 3)

            dve.sem_inc(c_x2, 2)
            IN_LINKS, OUT_LINKS = 5, 6

            def c_in_a(chain, i, s):
                t = pair(i, s)
                dve.wait_ge(c_in[s], (i + 1) * 32)
                chain.link(nc.vector.tensor_scalar(deg[:, s, :], acc_t[:, s, D:AW], 1.0, None, ALU.max))
                chain.link(nc.vector.reciprocal(rdeg[:, s, :], deg[:, s, :]))
                chain.link(nc.vector.scalar_tensor_tensor(
                    h0_t[:, s, :], acc_t[:, s, 0:D], rdeg[:, s, :], self_part[:, bass.ds(t * D, D)],
                    ALU.mult, ALU.add))
                chain.link(nc.vector.bn_stats(stats[:, s, :], h0_t[:, s, :]))
                hold(dve)
                nc.vector.bn_aggr(mean_var[:, s, :], stats[:, s, :]).then_inc(c_var, 1)

            def c_in_b(chain, i, s):
                dve.wait_ge(c_std, pair(i, s) + 1)
                chain.link(nc.vector.reciprocal(rstd[:, s, :], std[:, s, :]))
                nc.vector.tensor_scalar(shift[:, s, :], mean_var[:, s, 0:1], rstd[:, s, :], -1.0,
                                        ALU.mult, ALU.mult).then_inc(c_shift, 1)

            def c_out_c(chain, i, s):
                t = pair(i, s)
                y = y_t[:, s, :]
                dve.wait_ge(c_y, t + 1)
                chain.link(nc.vector.tensor_tensor(y, y, gamma_bc[:, :], ALU.mult))
                chain.link(nc.vector.tensor_tensor(y, y, beta_bc[:, :], ALU.add))
                chain.link(nc.vector.tensor_scalar(neg_t[:, 0, :], y, 0.0, alpha_bc[:, :], ALU.min, ALU.mult))
                chain.link(nc.vector.scalar_tensor_tensor(y, y, 0.0, neg_t[:, 0, :], ALU.max, ALU.add))
                dve.wait_ge(c_out_free, t + 1)
                dve.wait_ge(c_h2, t + 1)
                nc.vector.tensor_tensor(x2_t[:, s, :], y, res_c[:, s, :], ALU.add).then_inc(c_x2, 1)
                dve.wait_ge(c_x2, t + 3)
                chain.link(nc.vector.bn_stats(stats2[:, s, :], x2_t[:, s, :]))
                hold(dve)
                nc.vector.bn_aggr(mean_var2[:, s, :], stats2[:, s, :]).then_inc(c_var2, 1)

            def c_out_d(chain, i, s):
                dve.wait_ge(c_std2, pair(i, s) + 1)
                chain.link(nc.vector.reciprocal(rstd2[:, s, :], std2[:, s, :]))
                nc.vector.tensor_scalar(shift2[:, s, :], mean_var2[:, s, 0:1], rstd2[:, s, :], -1.0,
                                        ALU.mult, ALU.mult).then_inc(c_shift2, 1)

            def c_both(i, s, i1, s1):
                chain = Chain(dve, c_chain, pair(i, s) * (IN_LINKS + OUT_LINKS) + IN_LINKS)
                c_in_a(chain, i1, s1)
                c_out_c(chain, i, s)
                c_out_d(chain, i, s)
                c_in_b(chain, i1, s1)
                assert chain.n == IN_LINKS + OUT_LINKS

            chain = Chain(dve, c_chain)
            c_in_a(chain, 0, 0)
            c_in_b(chain, 0, 0)
            assert chain.n == IN_LINKS
            with dve.Fori(0, NT // 2) as i:
                c_both(i, 0, i, 1)
                c_both(i, 1, i + 1, 0)
            chain = Chain(dve, c_chain, (NT - 1) * (IN_LINKS + OUT_LINKS) + IN_LINKS)
            c_out_c(chain, NT // 2, 0)
            c_out_d(chain, NT // 2, 0)
            barrier(dve, 4)

            dve.wait_ge(s_dw, 7 * 16)
            silu_scale = SILU_2MOM * HID ** -0.5
            nc.vector.tensor_scalar(w4_sb[:, 0, 0:3 * MUL], w4_sb[:, 0, 0:3 * MUL], silu_scale, None, ALU.mult)
            nc.vector.tensor_scalar(w4_sb[:, 0, 3 * MUL:], w4_sb[:, 0, 3 * MUL:], silu_scale / math.sqrt(3.0),
                                    None, ALU.mult)
            nc.vector.tensor_scalar(wout_sb[:, :, :], wout_sb[:, :, :], (2 * MUL) ** -0.5 / AVG_NEIGHBORS,
                                    None, ALU.mult).then_inc(s_dw_scaled, 1)
            dve.sem_inc(dm.msg, TJ * dm.slots)
            dve.sem_inc(dx.msg, TJ * dx.slots)

            def messages(x_, g, s, k):
                for j in range(TJ):
                    T, b = k * TJ + j, j % 2
                    m, w = msg[:, b, :], psum[:, 1 + b, :]
                    row = rows_d[:, s, j * D:(j + 1) * D]
                    s0, s1 = row[:, 0:MUL], row[:, MUL:]
                    y = [attr[:, 0, bass.ds((g * TJ + j) * 4 + c, 1)] for c in range(4)]
                    q = q_t[:, b, :]
                    chain = Chain(dve, x_.q, T * 3)
                    nc.vector.tensor_scalar(q[:, 0:MUL], s1[:, 0:MUL], y[1], None, ALU.mult).then_inc(x_.q, 1)
                    dve.wait_ge(x_.weights, T + 1)
                    dve.wait_ge(x_.tile, T + 1)
                    nc.vector.scalar_tensor_tensor(
                        m[:, 2 * MUL:].rearrange("p (m c) -> p m c", m=3)[:, :, MUL:],
                        w[:, 2 * MUL:3 * MUL].unsqueeze(1).to_broadcast([P, 3, MUL]), y[0],
                        s1.rearrange("p (m c) -> p m c", m=3), ALU.mult, ALU.mult)
                    dve.wait_ge(x_.q, T * 3 + 1)
                    nc.vector.scalar_tensor_tensor(q[:, MUL:2 * MUL], s1[:, MUL:2 * MUL], y[2], q[:, 0:MUL],
                                                   ALU.mult, ALU.add).then_inc(x_.q, 1)
                    nc.vector.scalar_tensor_tensor(m[:, 0:MUL], w[:, 0:MUL], y[0], s0, ALU.mult, ALU.mult)
                    dve.wait_ge(x_.q, T * 3 + 2)
                    nc.vector.scalar_tensor_tensor(q[:, 2 * MUL:], s1[:, 2 * MUL:], y[3], q[:, MUL:2 * MUL],
                                                   ALU.mult, ALU.add).then_inc(x_.q, 1)
                    for c in range(3):
                        nc.vector.scalar_tensor_tensor(m[:, (2 + 2 * c) * MUL:(3 + 2 * c) * MUL],
                                                       w[:, MUL:2 * MUL], y[1 + c], s0, ALU.mult, ALU.mult)
                    dve.wait_ge(x_.q, T * 3 + 3)
                    nc.vector.tensor_tensor(m[:, MUL:2 * MUL], w[:, 3 * MUL:], q[:, 2 * MUL:], ALU.mult
                                            ).then_inc(x_.msg, 1)

            with dve.Fori(0, NG // D_SLOTS) as i:
                for s in range(D_SLOTS):
                    k = i * D_SLOTS + s
                    select(dm, sel_d, rel_main(k), s)
                    dve.wait_ge(dm.rows_in[s], (i + 1) * 16 * TJ)
                    messages(dm, k, s, k)
            barrier(dve, 5)

            def general_d(x_, g, w, k):
                rel_at = rel_of_window(x_, g, w, k)
                dve.wait_ge(x_.tile, k * TJ + 2)
                select(x_, sel_d, rel_at, 0)
                dve.wait_ge(x_.rows_in[0], (k + 1) * 16 * TJ)
                messages(x_, g, 0, k)
            general_pass(dve, dx, general_d)

        @block.tensor
        def _(pe):
            pe.wait_ge(s_const, 1)
            pe.wait_ge(s_w, 8 * 16)

            def a_step(i, s):
                t = pair(i, s)
                pe.wait_ge(a_h, t + 1)
                for c in range(KC):
                    last = nc.tensor.transpose(psum[:, s, c * P:(c + 1) * P], ht[:, s, c * P:(c + 1) * P],
                                               ident[:, :])
                last.then_inc(a_T, 1)
                pe.wait_ge(a_Tc, t + 1)
                pe.wait_ge(a_hn, t + 1)
                pe.wait_ge(a_self, t + 1)
                for w_sb, bank in ((wn_sb, 2), (ws_sb, 4)):
                    for c in range(KC):
                        last = nc.tensor.matmul(psum[:, bank + s, :], h_t[:, s, c * P:(c + 1) * P], w_sb[:, c, :],
                                                start=(c == 0), stop=(c == KC - 1))
                last.then_inc(a_mm, 1)

            with pe.Fori(0, NT // 2) as i:
                for s in range(2):
                    a_step(i, s)
            a_step(NT // 2, 0)
            barrier(pe, 1)

            pe.sem_inc(bm.summed, bm.slots)
            pe.sem_inc(bx.summed, bx.slots)

            def b_step(x_, i, s, s2, k):
                pe.wait_ge(x_.sel, k + 1)
                pe.wait_ge(x_.rows_in[s], (i + 1) * 16 * TJ)
                pe.wait_ge(x_.staged, k + 1)
                for j in range(TJ):
                    sel_j = sel_b[:, s, j * P:(j + 1) * P]
                    nc.tensor.matmul(psum[:, 2 * s2, :], sel_j, rows_b[:, s, j * D:(j + 1) * D],
                                     start=(j == 0), stop=(j == TJ - 1))
                    last = nc.tensor.matmul(psum[:, 2 * s2 + 1, 0:1], sel_j, ones[:, 0:1],
                                            start=(j == 0), stop=(j == TJ - 1))
                last.then_inc(x_.summed, 1)

            with pe.Fori(0, NG // B_SLOTS) as i:
                for s in range(B_SLOTS):
                    b_step(bm, i, s, s % 2, i * B_SLOTS + s)
            barrier(pe, 2)
            general_pass(pe, bx, lambda x_, g, w, k: b_step(x_, k, 0, 0, k))
            barrier(pe, 3)

            def c_step(i, s):
                t = pair(i, s)
                pe.wait_ge(c_h2, t + 3)
                h = h2_t[:, s, :]
                nc.tensor.transpose(psum[:, s, 0:P], h[:, 0:MUL], ident[:, :])
                for m in range(3):
                    last = nc.tensor.transpose(psum[:, s, (m + 1) * P:(m + 2) * P], h[:, MUL + m::3], ident[:, :])
                last.then_inc(c_T, 1)
                pe.wait_ge(c_Tc, t + 1)
                pe.wait_ge(c_upc, t + 1)
                for m in range(4):
                    last = nc.tensor.matmul(psum[:, 2 + s, m * MUL:(m + 1) * MUL], h2T_t[:, 0, m * P:(m + 1) * P],
                                            w_up[:, min(m, 1), :], start=True, stop=True)
                last.then_inc(c_up, 1)

            with pe.Fori(0, NT // 2) as i:
                for s in range(2):
                    c_step(i, s)
            c_step(NT // 2, 0)
            barrier(pe, 4)

            pe.wait_ge(s_dw_scaled, 1)
            pe.sem_inc(dm.tile, 2)
            pe.sem_inc(dx.tile, 2)
            pe.sem_inc(dm.T, 1)
            pe.sem_inc(dx.T, 1)
            pe.sem_inc(dm.o, 1)
            pe.sem_inc(dx.o, 1)

            def mlp(x_, n, i, s, k):
                if n == 0:
                    pe.wait_ge(x_.feat_in[s], (i + 1) * 16)
                    pe.wait_ge(x_.act[2], k + 1)
                    w, h = w1_sb[0:2 * BASIS, 0, :], feat_t[0:2 * BASIS, s, :]
                else:
                    pe.wait_ge(x_.act[n - 1], k + 1)
                    w, h = ((w2_sb[:, 0, :], h1[:, 0, :]), (w3_sb[:, 0, :], h2[:, 0, :]))[n - 1]
                nc.tensor.matmul(psum[:, 0, 0:HALF], w, h, start=True, stop=True).then_inc(x_.layer[n], 1)

            def edge_weights(x_, s, k, j):
                T = k * TJ + j
                if j == 0:
                    pe.wait_ge(x_.act[2], k + 2)
                pe.wait_ge(x_.msg, T - 1 + TJ * x_.slots)
                half, col = (j // 2) * HID, (j % 2) * P
                nc.tensor.matmul(psum[:, 1 + j % 2, :], h3[half:half + HID, s, col:col + P],
                                 w4_sb[half:half + HID, 0, :], start=True, stop=True).then_inc(x_.weights, 1)

            def sum_tile(x_, s, k, j):
                T = k * TJ + j
                pe.wait_ge(x_.msg, T + 1 + TJ * x_.slots)
                if j == 0:
                    pe.wait_ge(x_.sel, k + 1)
                    pe.wait_ge(x_.sum_copied, k + 1)
                for b in range(2):
                    last = nc.tensor.matmul(psum[:, 3 + b, :], sel_d[:, s, j * P:(j + 1) * P],
                                            msg[:, j % 2, b * D:(b + 1) * D], start=(j == 0), stop=(j == TJ - 1))
                last.then_inc(x_.tile, 1)

            def transpose_sum(x_, k):
                pe.wait_ge(x_.sum_copied, k + 2)
                pe.wait_ge(x_.T_copied, k + 1)
                for c in range(8):
                    last = nc.tensor.transpose(psum[:, 5 + c // 4, (c % 4) * P:(c % 4 + 1) * P],
                                               sum_sb[:, 0, c * P:(c + 1) * P], ident[:, :])
                last.then_inc(x_.T, 1)

            def output_maps(x_, k):
                pe.wait_ge(x_.T_copied, k + 2)
                pe.wait_ge(x_.staged, k + x_.bufs)
                for m in range(4):
                    for c in range(2):
                        last = nc.tensor.matmul(psum[:, 7, m * MUL:(m + 1) * MUL],
                                                sumT_sb[:, 0, (2 * m + c) * P:(2 * m + c + 1) * P],
                                                wout_sb[:, 2 * min(m, 1) + c, :], start=(c == 0), stop=(c == 1))
                last.then_inc(x_.o, 1)

            def d_step(i, s, first=False, last=False):
                k = pair(i, s)
                i1, s1 = (i, 1) if s == 0 else (i + 1, 0)
                edge_weights(dm, s, k, 0)
                edge_weights(dm, s, k, 1)
                if not first:
                    transpose_sum(dm, k - 1)
                sum_tile(dm, s, k, 0)
                edge_weights(dm, s, k, 2)
                if not last:
                    mlp(dm, 0, i1, s1, k + 1)
                sum_tile(dm, s, k, 1)
                edge_weights(dm, s, k, 3)
                if not last:
                    mlp(dm, 1, i1, s1, k + 1)
                sum_tile(dm, s, k, 2)
                if not first:
                    output_maps(dm, k - 1)
                if not last:
                    mlp(dm, 2, i1, s1, k + 1)
                sum_tile(dm, s, k, 3)

            for n in range(3):
                mlp(dm, n, 0, 0, 0)
            d_step(0, 0, first=True)
            d_step(0, 1)
            with pe.Fori(1, NG // 2 - 1) as i:
                d_step(i, 0)
                d_step(i, 1)
            d_step(NG // 2 - 1, 0)
            d_step(NG // 2 - 1, 1, last=True)
            transpose_sum(dm, NG - 1)
            output_maps(dm, NG - 1)
            barrier(pe, 5)

            def general_d(x_, g, w, k):
                for n in range(3):
                    mlp(x_, n, k, 0, k)
                for j in range(TJ):
                    edge_weights(x_, 0, k, j)
                    sum_tile(x_, 0, k, j)
                transpose_sum(x_, k)
                output_maps(x_, k)
            general_pass(pe, dx, general_d)


def kernel(x, src, dst, edge_attr_4, edge_attr_8, L0_gnn_W_self, L0_gnn_b_self, L0_gnn_W_neigh, L0_gnn_gamma,
           L0_gnn_beta, L0_gnn_alpha, L1_gnn_W_up0, L1_gnn_W_up1, L1_gnn_W_mlp1, L1_gnn_W_mlp2, L1_gnn_W_mlp3,
           L1_gnn_W_mlp4, L1_gnn_W_out0, L1_gnn_W_out1):
    import concourse.bacc as bacc
    from concourse.bass_utils import run_bass_kernel_spmd

    a = np.asarray
    n_pad = NG * GE - N_EDGES

    def edge_pad(v):
        return np.concatenate([a(v), np.repeat(a(v)[-1:], n_pad, axis=0)])

    def to_rows(v):
        return np.ascontiguousarray(np.broadcast_to(a(v).reshape(1, -1), (P, a(v).size)))

    def columns(v):
        return np.ascontiguousarray(v.reshape(NG, TJ, P, -1).transpose(2, 0, 1, 3).reshape(P, -1))

    def block_diagonal(w):
        w = a(w)
        both = np.zeros((2 * w.shape[0], 2 * w.shape[1]), w.dtype)
        both[:w.shape[0], :w.shape[1]] = w
        both[w.shape[0]:, w.shape[1]:] = w
        return both

    x_pad = np.zeros((NP, D), a(x).dtype)
    x_pad[:N_NODES] = a(x)
    src_p, dst_p = edge_pad(src), edge_pad(dst)
    ins = {
        "x": x_pad,
        "src_g": np.ascontiguousarray(src_p.reshape(NG, TJ, P).transpose(0, 2, 1)),
        "dst_rows": dst_p.reshape(GP, 2 * GE),
        "dst_cols": columns(dst_p),
        "attr_cols": columns(edge_pad(edge_attr_4)),
        "feat_g": np.ascontiguousarray(edge_pad(edge_attr_8).reshape(NG, 2, HALF, BASIS).transpose(0, 1, 3, 2)
                                       .reshape(NG, 2 * BASIS, HALF)),
        "w_self": a(L0_gnn_W_self), "w_neigh": a(L0_gnn_W_neigh),
        "b_self": to_rows(L0_gnn_b_self), "gamma": to_rows(L0_gnn_gamma), "beta": to_rows(L0_gnn_beta),
        "alpha": to_rows(L0_gnn_alpha),
        "w_up0": a(L1_gnn_W_up0), "w_up1": a(L1_gnn_W_up1),
        "w_mlp1": block_diagonal(L1_gnn_W_mlp1), "w_mlp2": block_diagonal(L1_gnn_W_mlp2),
        "w_mlp3": block_diagonal(L1_gnn_W_mlp3),
        "w_mlp4": np.concatenate([a(L1_gnn_W_mlp4)] * 2),
        "w_out0": a(L1_gnn_W_out0), "w_out1": a(L1_gnn_W_out1),
    }
    nc = bacc.Bacc("TRN2", target_bir_lowering=False, num_devices=1)
    aps = {name: nc.dram_tensor(f"in_{name}", v.shape, mybir.dt.from_np(v.dtype), kind="ExternalInput").ap()
           for name, v in ins.items()}
    out = nc.dram_tensor("out_0", (WINDOW_ROWS, D), F32, kind="ExternalOutput").ap()
    gnn_kernel(nc, *aps.values(), out)
    r = run_bass_kernel_spmd(nc, [{f"in_{name}": v for name, v in ins.items()}], core_ids=[0])
    return r.results[0]["out_0"][:N_NODES]
```

```python
import math
from contextlib import ExitStack

import numpy as np
import concourse.bass as bass
from concourse import mybir

F32 = mybir.dt.float32
F32R = mybir.dt.float32r
I32 = mybir.dt.int32
ALU = mybir.AluOpType
ACT = mybir.ActivationFunctionType
AX = mybir.AxisListType

P = 128
N_NODES, D = 6250, 512
N_EDGES = 100000
KC = D // P
NT = -(-N_NODES // P)
NP = NT * P
WINDOW_ROWS = NP + P
TJ = 4
GE = TJ * P
NG = -(-N_EDGES // GE)
MUL = 128
HID = 64
BASIS = 8
HALF = GE // 2
LN_EPS = 1e-5
SILU_2MOM = 1.679177
AVG_NEIGHBORS = 10.0
AW = D + 1
B_SLOTS, B_LAG = 4, 3
D_SLOTS, D_LAG = 4, 4
RING = TJ
MSG_AHEAD = 2
V_COLS = 5 * MUL
DEAD = -1.0e6
assert NG % B_SLOTS == 0 and NG == NT * B_SLOTS and NG % D_SLOTS == 0 and NG % 2 == 0 and NT % 2 == 1
GP = NG // 2


def gnn_kernel(nc, x, src_g, dst_rows, dst_cols, attr_cols, feat_g, w_self, w_neigh, b_self, gamma, beta,
               alpha, w_up0, w_up1, w_mlp1, w_mlp2, w_mlp3, w_mlp4, w_out0, w_out1, out):
    table0 = nc.dram_tensor("table0", (NP, D), F32, kind="Internal").ap()
    table1 = nc.dram_tensor("table1", (NP, D), F32, kind="Internal").ap()
    resid = nc.dram_tensor("resid", (NP, D), F32, kind="Internal").ap()
    acc0 = nc.dram_tensor("acc0", (WINDOW_ROWS, AW), F32, kind="Internal").ap()
    meta = nc.dram_tensor("meta", (2, NG), I32, kind="Internal").ap()

    with ExitStack() as ctx:
        def sb(name, shape, dt=F32):
            return ctx.enter_context(nc.sbuf_tensor(name, shape, dt))

        def sem(name):
            return ctx.enter_context(nc.semaphore(name))

        def carve(arena, sizes):
            views, at = [], 0
            for shape in sizes:
                n = math.prod(shape)
                v = arena[:, at:at + n]
                if len(shape) == 2:
                    v = v.rearrange("p (a b) -> p a b", a=shape[0])
                if len(shape) == 3:
                    v = v.rearrange("p (a b c) -> p a b c", a=shape[0], b=shape[1])
                views.append(v)
                at += n
            assert at <= arena.shape[1], (at, arena.shape)
            return views

        big = sb("big", [P, NT * D])
        sel = sb("sel", [P, 4, TJ * P], F32R)
        hi = sb("hi", [P, RING, 8 * MUL], F32R)
        lo = sb("lo", [P, RING, 8 * MUL], F32R)
        ones = sb("ones", [P, 2], F32R)
        work = sb("work", [P, 2 * KC * D + 10 * D])
        self_part = big
        bias_bc, gamma_bc, beta_bc = sb("bias_bc", [P, D]), sb("gamma_bc", [P, D]), sb("beta_bc", [P, D])
        alpha_bc = sb("alpha_bc", [P, 1])
        eps_t = sb("eps_t", [P, 1])
        ident = sb("ident", [P, P])
        iota_n = sb("iota_n", [P, P])
        window_start = sb("window_start", [P, NT])
        rel = sb("rel", [P, NG * TJ])
        rel_w = sb("rel_w", [P, TJ])
        src_idx = [sb(f"src_idx{s}", [P, TJ], I32) for s in range(B_SLOTS)]
        meta_row = sb("meta_row", [1, 4 * NG], I32)
        START, MORE, BEFORE = 0, NG, 2 * NG
        stats = sb("stats", [P, 2, 6])
        mean_var = sb("mean_var", [P, 2, 2])
        std = sb("std", [P, 2, 1])
        rstd = sb("rstd", [P, 2, 1])
        shift = sb("shift", [P, 2, 1])
        stats2 = sb("stats2", [P, 2, 6])
        mean_var2 = sb("mean_var2", [P, 2, 2])
        std2 = sb("std2", [P, 2, 1])
        rstd2 = sb("rstd2", [P, 2, 1])
        shift2 = sb("shift2", [P, 2, 1])
        deg = sb("deg", [P, 2, 1])
        rdeg = sb("rdeg", [P, 2, 1])
        w_up = sb("w_up", [P, 2, MUL])

        ws_sb, wn_sb, xt, ht, h_t, hn_t, res_t = carve(
            work, [(KC, D), (KC, D), (2, D), (2, D), (2, D), (2, D), (2, D)])
        _, hT_b, stage_b, rows_in_work = carve(work, [(KC, D), (1, D), (2, AW), (2, TJ * D)])
        rows_alone = sb("rows_alone", [P, B_SLOTS - 2, TJ * D])
        rows = [rows_alone[:, 0, :], rows_alone[:, 1, :], rows_in_work[:, 0, :], rows_in_work[:, 1, :]]
        hi_b = hi[:, :, :].rearrange("p a (b n) -> p (a b) n", b=2)
        lo_b = lo[:, :, :].rearrange("p a (b n) -> p (a b) n", b=2)
        acc_t, res_c, h0_t, y_t, neg_t, x2_t, h2_t, h2T_t, up_t = carve(
            work, [(2, AW), (2, D), (2, D), (2, D), (1, D), (2, D), (2, D), (1, D), (2, D)])
        (prod, u_t, q_t, feat_t, h1, h2, h3, sum_sb, sumT_sb, o_sb, attr, w1_sb, w2_sb, w3_sb, w4_sb,
         wout_sb) = carve(
            big, [(RING, 8 * MUL), (RING, MUL), (RING, 3 * MUL), (D_SLOTS, HALF),
                  (1, HALF), (1, HALF), (2, HALF), (1, 8 * MUL), (1, 8 * MUL), (2, 4 * MUL),
                  (1, NG * TJ * 4), (1, P), (1, P), (1, P), (1, D), (4, MUL)])
        _, dst_r, dst_c, start_c = carve(big, [(AW,), (2 * GE,), (NG * TJ,), (NG,)])
        dst_r_i, dst_c_i, start_bc = dst_r[0:GP, :].bitcast(I32), dst_c.bitcast(I32), start_c.bitcast(I32)
        least = sb("least", [GP, 2], I32)
        more = sb("more", [GP, 2], I32)
        more_f = sb("more_f", [1, NG])
        zero_f = sb("zero_f", [1, NG])
        prefix_f = sb("prefix_f", [1, NG])

        psum = ctx.enter_context(nc.psum_tensor("psum", [P, 8, D], F32))
        flat = psum[:, :, :].rearrange("p b n -> p (b n)")

        s_bar = sem("s_barrier")
        s_held = sem("s_waits_held")
        s_w = sem("s_weights_in")
        s_dst = sem("s_dst_in")
        s_const = sem("s_constants_made")
        s_pool_const = sem("s_pool_constants")
        s_meta_made = sem("s_meta_made")
        s_meta_out = sem("s_meta_out")
        s_meta_in = sem("s_meta_in")
        s_setup = sem("s_setup_chain")
        s_zero = sem("s_zero_rows")
        s_zeroed = sem("s_zero_tile")

        ENGINES = 5

        def barrier(eng, n):
            eng.drain().then_inc(s_bar, 1)
            eng.wait_ge(s_bar, ENGINES * n)

        def hold(eng):
            eng.sem_inc(s_held, 1)

        class Chain:
            def __init__(self, eng, s, base=0):
                self.eng, self.s, self.base, self.n = eng, s, base, 0

            def link(self, ins):
                self.n += 1
                ins.then_inc(self.s, 1)
                self.eng.wait_ge(self.s, self.base + self.n)

        def pair(r, s):
            return r * 2 + s

        a_x_in = [sem(f"a_x_in{s}") for s in range(2)]
        a_chain = sem("a_vector_chain")
        a_var = sem("a_variance")
        a_std = sem("a_std")
        a_shift = sem("a_shift")
        a_h = sem("a_h_ready")
        a_T = sem("a_h_transposed")
        a_Tc = sem("a_h_transposed_copied")
        a_mm = sem("a_products")
        a_hn = sem("a_neigh_copied")
        a_kept = sem("a_transposed_kept")
        a_res = sem("a_resid_made")
        a_res_out = sem("a_resid_out")
        a_hn_out = sem("a_table_out")
        a_out_free = sem("a_stored")

        class EdgeSemsB:
            def __init__(self, name, slots):
                self.slots = slots
                self.idx_in = [sem(f"{name}_idx_in{s}") for s in range(slots)]
                self.rows_in = [sem(f"{name}_rows_in{s}") for s in range(slots)]
                self.sel = sem(f"{name}_selection_made")
                self.hi = sem(f"{name}_hi")
                self.lo = sem(f"{name}_lo")
                self.relw = sem(f"{name}_rel_window")
                self.bufs = min(2, slots)
                self.summed = sem(f"{name}_summed")
                self.staged = sem(f"{name}_staged")
                self.stage_free = sem(f"{name}_stage_free")
                self.added = sem(f"{name}_added")

        bm = EdgeSemsB("b", B_SLOTS)
        bx = EdgeSemsB("bx", 1)
        b_hT = sem("b_hT_taken")
        b_self_mm = sem("b_self_product")
        b_kept = sem("b_self_kept")

        c_in = [sem(f"c_in{s}") for s in range(2)]
        c_chain = sem("c_vector_chain")
        c_var, c_std, c_shift, c_y = sem("c_var"), sem("c_std"), sem("c_shift"), sem("c_y")
        c_var2, c_std2, c_shift2 = sem("c_var2"), sem("c_std2"), sem("c_shift2")
        c_x2 = sem("c_x2_made")
        c_h2 = sem("c_h2_made")
        c_T, c_Tc, c_up = sem("c_h2_transposed"), sem("c_h2_transposed_copied"), sem("c_up_products")
        c_upc = sem("c_up_copied")
        c_affine = sem("c_affine")
        c_x2_out, c_up_out = sem("c_x2_out"), sem("c_table_out")
        c_x2_free = sem("c_x2_stored")
        c_up_free = sem("c_up_stored")

        class EdgeSemsD:
            def __init__(self, name, slots):
                self.slots = slots
                self.bufs = min(2, slots)
                self.feat_in = [sem(f"{name}_feat_in{s}") for s in range(slots)]
                self.idx_in = [sem(f"{name}_idx_in{s}") for s in range(slots)]
                self.rows_in = [sem(f"{name}_rows_in{s}") for s in range(slots)]
                self.relw = sem(f"{name}_rel_window")
                self.sel = sem(f"{name}_selection_made")
                self.layer = [sem(f"{name}_layer{n}") for n in range(3)]
                self.act = [sem(f"{name}_layer{n}_silu") for n in range(3)]
                self.weights = sem(f"{name}_edge_weights")
                self.q = sem(f"{name}_q_chain")
                self.prod = sem(f"{name}_products")
                self.p2 = sem(f"{name}_p2_chain")
                self.hi = sem(f"{name}_hi")
                self.lo_v = sem(f"{name}_lo_vector")
                self.lo_p = sem(f"{name}_lo_gpsimd")
                self.tile = sem(f"{name}_tile_summed")
                self.sum_copied = sem(f"{name}_sum_copied")
                self.T = sem(f"{name}_sum_transposed")
                self.T_copied = sem(f"{name}_sum_transposed_copied")
                self.o = sem(f"{name}_output_maps")
                self.staged = sem(f"{name}_staged")
                self.stage_free = sem(f"{name}_stage_free")
                self.added = sem(f"{name}_added")

        dm = EdgeSemsD("d", D_SLOTS)
        dx = EdgeSemsD("dx", 1)
        s_dw = sem("d_weights_in")
        s_dw_scaled = sem("d_weights_scaled")

        def general_pass(eng, x, step):
            any_more = eng.value_load(meta_row[0:1, 3 * NG:3 * NG + 1], min_val=0, max_val=NG * NT)
            with eng.If(any_more > 0):
                with eng.Fori(0, NG) as g:
                    n_more = eng.value_load(meta_row[0:1, bass.ds(g + MORE, 1)], min_val=0, max_val=NT - 1)
                    before = eng.value_load(meta_row[0:1, bass.ds(g + BEFORE, 1)], min_val=0, max_val=NG * NT)
                    with eng.If(n_more > 0):
                        with eng.Fori(0, n_more) as w:
                            step(x, g, w + 1, before + w)
                    eng.nop()
            eng.nop()

        block = ctx.enter_context(nc.Block())

        @block.sync
        def _(sp):
            sp.dma_start(dst_r_i[:, :], dst_rows).then_inc(s_dst, 16)
            sp.dma_start(dst_c_i[:, :], dst_cols).then_inc(s_dst, 16)
            sp.dma_start(wn_sb, w_neigh.rearrange("(c p) n -> p c n", p=P)).then_inc(s_w, 16)
            sp.dma_start(ws_sb, w_self.rearrange("(c p) n -> p c n", p=P)).then_inc(s_w, 16)
            sp.dma_start(bias_bc[:, :], b_self).then_inc(s_w, 16)
            sp.dma_start(gamma_bc[:, :], gamma).then_inc(s_w, 16)
            sp.dma_start(beta_bc[:, :], beta).then_inc(s_w, 16)
            sp.dma_start(alpha_bc[:, :], alpha).then_inc(s_w, 16)
            sp.dma_start(w_up[:, 0, :], w_up0).then_inc(s_w, 16)
            sp.dma_start(w_up[:, 1, :], w_up1).then_inc(s_w, 16)

            def load_x(i, s):
                t = pair(i, s)
                sp.wait_ge(a_res, t + 1)
                sp.dma_start(xt[:, s, :], x[bass.ds(t * P, P), :]).then_inc(a_x_in[s], 16)

            sp.wait_ge(s_meta_made, 1)
            sp.dma_start(meta[0, :].rearrange("(p c) -> p c", c=2), least[:, :]).then_inc(s_meta_out, 16)
            sp.dma_start(meta[1, :].rearrange("(p c) -> p c", c=2), more[:, :]).then_inc(s_meta_out, 16)
            sp.wait_ge(s_meta_out, 32)
            sp.dma_start(meta_row[0:1, 0:2 * NG], meta.rearrange("(a r) g -> a (r g)", a=1)).then_inc(s_meta_in, 16)
            sp.dma_start(start_bc[:, :], meta[0, :].partition_broadcast(P)).then_inc(s_meta_in, 16)

            with sp.Fori(0, NT // 2) as i:
                for s in range(2):
                    load_x(i, s)
            load_x(NT // 2, 0)
            sp.wait_ge(s_zeroed, 1)
            barrier(sp, 1)

            def idx_b(x_, g, i, s, k):
                sp.wait_ge(x_.summed, k + 1)
                sp.dma_start(src_idx[s][:, :], src_g[bass.ds(g, 1), :, :].rearrange("a p j -> (a p) j")
                             ).then_inc(x_.idx_in[s], 16)

            with sp.Fori(0, NG // B_SLOTS) as i:
                for s in range(B_SLOTS):
                    k = i * B_SLOTS + s
                    idx_b(bm, k, i, s, k)
            barrier(sp, 2)
            general_pass(sp, bx, lambda x_, g, w, k: idx_b(x_, g, k, 0, k))
            barrier(sp, 3)

            def load_c(i, s):
                t = pair(i, s)
                sp.wait_ge(c_x2, t + 1)
                sp.dma_start(acc_t[:, s, :], acc0[bass.ds(t * P, P), :]).then_inc(c_in[s], 16)
                sp.dma_start(res_c[:, s, :], resid[bass.ds(t * P, P), :]).then_inc(c_in[s], 16)

            with sp.Fori(0, NT // 2) as i:
                for s in range(2):
                    load_c(i, s)
            load_c(NT // 2, 0)
            barrier(sp, 4)

            sp.dma_start(attr[:, 0, :], attr_cols).then_inc(s_dw, 16)
            sp.dma_start(w1_sb[0:2 * BASIS, 0, :], w_mlp1).then_inc(s_dw, 16)
            sp.dma_start(w2_sb[:, 0, :], w_mlp2).then_inc(s_dw, 16)
            sp.dma_start(w3_sb[:, 0, :], w_mlp3).then_inc(s_dw, 16)
            sp.dma_start(w4_sb[:, 0, :], w_mlp4).then_inc(s_dw, 16)
            sp.dma_start(wout_sb[:, 0:2, :], w_out0.rearrange("(c p) n -> p c n", p=P)).then_inc(s_dw, 16)
            sp.dma_start(wout_sb[:, 2:4, :], w_out1.rearrange("(c p) n -> p c n", p=P)).then_inc(s_dw, 16)

            def inputs_d(x_, g, s, k):
                sp.wait_ge(x_.prod, (k + 1) * TJ)
                sp.dma_start(src_idx[s][:, :], src_g[bass.ds(g, 1), :, :].rearrange("a p j -> (a p) j")
                             ).then_inc(x_.idx_in[s], 16)
                sp.dma_start(feat_t[0:2 * BASIS, s, :], feat_g[bass.ds(g, 1), :, :].rearrange("a f e -> (a f) e")
                             ).then_inc(x_.feat_in[s], 16)

            with sp.Fori(0, NG // D_SLOTS) as i:
                for s in range(D_SLOTS):
                    k = i * D_SLOTS + s
                    inputs_d(dm, k, s, k)
            barrier(sp, 5)
            general_pass(sp, dx, lambda x_, g, w, k: inputs_d(x_, g, 0, k))

        @block.gpsimd
        def _(pool):
            nc.gpsimd.memset(ident[:, :], 0.0).then_inc(s_pool_const, 1)
            nc.gpsimd.memset(ones[:, :].bitcast(F32), 1.0)
            nc.gpsimd.memset(eps_t[:, :], LN_EPS)
            nc.gpsimd.iota(iota_n[:, :], pattern=[[1, P]], base=0, channel_multiplier=0,
                           allow_small_or_imprecise_dtypes=True)
            nc.gpsimd.iota(window_start[:, :], pattern=[[P, NT]], base=0, channel_multiplier=0,
                           allow_small_or_imprecise_dtypes=True)
            pool.wait_ge(s_pool_const, 1)
            nc.gpsimd.affine_select(out=ident[:, :], in_=ident[:, :], compare_op=ALU.not_equal, fill=1.0,
                                    base=0, pattern=[[-1, P]], channel_multiplier=1).then_inc(s_const, 1)

            pool.wait_ge(s_zeroed, 1)
            with pool.Fori(0, WINDOW_ROWS // P) as t:
                pool.dma_start(acc0[bass.ds(t * P, P), :], big[:, 0:AW]).then_inc(s_zero, 16)
            pool.dma_start(out[NP:WINDOW_ROWS, :], big[:, 0:D]).then_inc(s_zero, 16)
            pool.wait_ge(s_zero, 16 * (WINDOW_ROWS // P + 1))

            pool.sem_inc(a_out_free, 2)

            def store_a(i, s):
                t = pair(i, s)
                pool.wait_ge(a_res, t + 3)
                hold(pool)
                pool.dma_start(resid[bass.ds(t * P, P), :], res_t[:, s, :]).then_inc(a_res_out, 16)
                pool.wait_ge(a_hn, t + 3)
                hold(pool)
                pool.dma_start(table0[bass.ds(t * P, P), :], hn_t[:, s, :]).then_inc(a_hn_out, 16)
                pool.wait_ge(a_res_out, t * 16 + 16)
                pool.wait_ge(a_hn_out, t * 16 + 16)
                pool.sem_inc(a_out_free, 1)

            with pool.Fori(0, NT // 2) as i:
                for s in range(2):
                    store_a(i, s)
            store_a(NT // 2, 0)
            barrier(pool, 1)

            def gather_waits(x_, i, s, k, rows_free, per_step):
                pool.wait_ge(x_.idx_in[s], (i + 1) * 16)
                pool.wait_ge(rows_free, (k + 1) * per_step)
                hold(pool)

            def gather_tile(x_, table, s, j):
                nc.gpsimd.indirect_dma_start(
                    rows[s][:, j * D:(j + 1) * D], None, table,
                    bass.IndirectOffsetOnAxis(ap=src_idx[s][:, j:j + 1], axis=0)).then_inc(x_.rows_in[s], 16)

            def add_window(x_, target, stage, g, s, k, first=False):
                row = pool.value_load(meta_row[0:1, bass.ds(g + START, 1)], min_val=0, max_val=N_NODES - 1)
                pool.wait_ge(x_.staged, k + 1 + x_.bufs)
                if first:
                    hold(pool)
                else:
                    pool.wait_ge(x_.added, k * 16)
                    pool.sem_inc(x_.stage_free, 1)
                pool.dma_start(target[bass.ds(row, P), :], stage[:, s, :], accum_op=ALU.add
                               ).then_inc(x_.added, 16)

            def add_window_alone(x_, target, stage, g, w, k):
                row0 = pool.value_load(meta_row[0:1, bass.ds(g + START, 1)], min_val=0, max_val=N_NODES - 1)
                row = nc.s_assert_within(row0 + w * P, 0, WINDOW_ROWS - P)
                pool.wait_ge(x_.staged, k + 1 + x_.bufs)
                hold(pool)
                pool.dma_start(target[bass.ds(row, P), :], stage[:, 0, :], accum_op=ALU.add
                               ).then_inc(x_.added, 16)
                pool.wait_ge(x_.added, (k + 1) * 16)
                pool.sem_inc(x_.stage_free, 1)

            def steps_ahead(first_i, step):
                for k in range(first_i * 4):
                    step(k // 4, k % 4)
                with pool.Fori(first_i, NG // 4) as i:
                    for s in range(4):
                        step(i, s)

            pool.sem_inc(bm.stage_free, bm.bufs)
            pool.sem_inc(bx.stage_free, bx.bufs)

            def step_b(i, s):
                k = i * B_SLOTS + s
                if not isinstance(k, int) or k >= B_LAG:
                    add_window(bm, acc0, stage_b, k - B_LAG, (s - B_LAG) % 2, k - B_LAG,
                               first=isinstance(k, int) and k == B_LAG)
                gather_waits(bm, i, s, k, bm.summed, 1)
                for j in range(TJ):
                    gather_tile(bm, table0, s, j)

            steps_ahead(1, step_b)
            for k in range(NG - B_LAG, NG):
                add_window(bm, acc0, stage_b, k, k % 2, k)
            pool.wait_ge(bm.added, NG * 16)
            barrier(pool, 2)

            def general_b(x_, g, w, k):
                gather_waits(x_, k, 0, k, x_.summed, 1)
                for j in range(TJ):
                    gather_tile(x_, table0, 0, j)
                add_window_alone(x_, acc0, stage_b, g, w, k)
            general_pass(pool, bx, general_b)
            barrier(pool, 3)

            pool.sem_inc(c_x2_free, 2)
            pool.sem_inc(c_up_free, 2)

            def affine_c(t, s):
                for n in range(2):
                    pool.wait_ge(c_y, t + 1) if n == 0 else pool.wait_ge(c_affine, t * 2 + 1)
                    nc.gpsimd.tensor_tensor(y_t[:, s, :], y_t[:, s, :], (gamma_bc, beta_bc)[n][:, :],
                                            (ALU.mult, ALU.add)[n]).then_inc(c_affine, 1)

            def store_x2(t, s, first=False):
                if not first:
                    pool.wait_ge(c_x2_out, t * 16)
                    pool.sem_inc(c_x2_free, 1)
                pool.wait_ge(c_x2, t + 3)
                hold(pool)
                pool.dma_start(out[bass.ds(t * P, P), :], x2_t[:, s, :]).then_inc(c_x2_out, 16)

            def store_up(t, s, first=False):
                if not first:
                    pool.wait_ge(c_up_out, t * 16)
                    pool.sem_inc(c_up_free, 1)
                pool.wait_ge(c_upc, t + 3)
                hold(pool)
                pool.dma_start(table1[bass.ds(t * P, P), :], up_t[:, s, :]).then_inc(c_up_out, 16)

            affine_c(0, 0)
            affine_c(1, 1)
            store_x2(0, 0, first=True)
            affine_c(2, 0)
            store_x2(1, 1)
            store_up(0, 0, first=True)
            with pool.Fori(1, NT // 2) as i:
                affine_c(i * 2 + 1, 1)
                store_x2(i * 2, 0)
                store_up(i * 2 - 1, 1)
                affine_c(i * 2 + 2, 0)
                store_x2(i * 2 + 1, 1)
                store_up(i * 2, 0)
            store_x2(NT - 1, 0)
            store_up(NT - 2, 1)
            store_up(NT - 1, 0)
            pool.wait_ge(c_x2_out, NT * 16)
            pool.wait_ge(c_up_out, NT * 16)
            barrier(pool, 4)

            pool.sem_inc(dm.stage_free, dm.bufs)
            pool.sem_inc(dx.stage_free, dx.bufs)
            pool.sem_inc(dm.lo_p, RING)
            pool.sem_inc(dx.lo_p, RING)

            def lo_tile(x_, k, j):
                T, b = k * TJ + j, j
                pool.wait_ge(x_.hi, T + 1)
                nc.gpsimd.tensor_tensor(lo[:, b, V_COLS:], prod[:, b, V_COLS:], hi[:, b, V_COLS:].bitcast(F32),
                                        ALU.subtract).then_inc(x_.lo_p, 1)

            def step_d(i, s):
                k = i * D_SLOTS + s
                known = isinstance(k, int)
                gather_waits(dm, i, s, k, dm.prod, TJ)
                for j in range(TJ):
                    gather_tile(dm, table1, s, j)
                    if not known or k >= MSG_AHEAD:
                        lo_tile(dm, k - MSG_AHEAD, j)
                if not known or k >= D_LAG:
                    add_window(dm, out, o_sb, k - D_LAG, (s - D_LAG) % 2, k - D_LAG, first=known and k == D_LAG)

            steps_ahead(2, step_d)
            for k in range(NG, NG + D_LAG):
                if k - MSG_AHEAD < NG:
                    for j in range(TJ):
                        lo_tile(dm, k - MSG_AHEAD, j)
                add_window(dm, out, o_sb, k - D_LAG, (k - D_LAG) % 2, k - D_LAG)
            pool.wait_ge(dm.added, NG * 16)
            barrier(pool, 5)

            def general_d(x_, g, w, k):
                gather_waits(x_, k, 0, k, x_.prod, TJ)
                for j in range(TJ):
                    gather_tile(x_, table1, 0, j)
                for j in range(TJ):
                    lo_tile(x_, k, j)
                add_window_alone(x_, out, o_sb, g, w, k)
            general_pass(pool, dx, general_d)

        @block.scalar
        def _(act):
            act.wait_ge(s_const, 1)
            act.sem_inc(a_hn, 2)

            def a_front(i, s):
                t = pair(i, s)
                act.wait_ge(a_var, t + 1)
                nc.scalar.activation(std[:, s, :], mean_var[:, s, 1:2], ACT.Sqrt, bias=eps_t[:, :]
                                     ).then_inc(a_std, 1)
                act.wait_ge(a_shift, t + 1)
                act.wait_ge(a_res, t + 1)
                nc.scalar.activation(ht[:, s, :], xt[:, s, :], ACT.Relu, bias=shift[:, s, :],
                                     scale=rstd[:, s, :]).then_inc(a_h, 1)

            def a_back(i, s):
                t = pair(i, s)
                act.wait_ge(a_T, t + 1)
                act.wait_ge(a_kept, t + 1)
                nc.scalar.activation(h_t[:, s, :], psum[:, s, :], ACT.Copy).then_inc(a_Tc, 1)
                act.wait_ge(a_mm, t + 1)
                act.wait_ge(a_out_free, t + 1)
                nc.scalar.activation(hn_t[:, s, :], psum[:, 2 + s, :], ACT.Copy).then_inc(a_hn, 1)

            a_front(0, 0)
            with act.Fori(0, NT // 2) as i:
                a_front(i, 1)
                a_back(i, 0)
                a_front(i + 1, 0)
                a_back(i, 1)
            a_back(NT // 2, 0)
            barrier(act, 1)

            act.sem_inc(bm.staged, bm.bufs)
            act.sem_inc(bx.staged, bx.bufs)

            def b_hi(x_, i, s, k):
                act.wait_ge(x_.rows_in[s], (i + 1) * 16 * TJ)
                two = x_.bufs == 2
                act.wait_ge(x_.summed, k + x_.slots - 1 if two else k + 1)
                for j in range(TJ):
                    nc.scalar.activation(hi_b[:, (s % x_.bufs) * TJ + j, :], rows[s][:, j * D:(j + 1) * D], ACT.Copy
                                         ).then_inc(x_.hi, 1)

            def b_stage(x_, s2, k):
                act.wait_ge(x_.summed, k + 1 + x_.slots)
                act.wait_ge(x_.stage_free, k + 1)
                nc.scalar.activation(stage_b[:, s2, :], flat[:, 2 * s2 * D:2 * s2 * D + AW], ACT.Copy
                                     ).then_inc(x_.staged, 1)

            def b_round(i, last=False):
                for s in range(B_SLOTS):
                    k = i * B_SLOTS + s
                    if s == 1:
                        act.wait_ge(b_kept, i + 1)
                        nc.scalar.activation(hT_b[:, 0, :], big[:, bass.ds(i * D, D)], ACT.Copy).then_inc(b_hT, 1)
                    if s < B_SLOTS - 1:
                        b_hi(bm, i, s + 1, k + 1)
                    elif not last:
                        b_hi(bm, i + 1, 0, k + 1)
                    b_stage(bm, s % 2, k)

            b_hi(bm, 0, 0, 0)
            with act.Fori(0, NT - 1) as i:
                b_round(i)
            b_round(NT - 1, last=True)
            barrier(act, 2)

            def general_b(x_, g, w, k):
                b_hi(x_, k, 0, k)
                b_stage(x_, 0, k)
            general_pass(act, bx, general_b)
            barrier(act, 3)

            act.sem_inc(c_h2, 2)
            act.sem_inc(c_upc, 2)

            def c_std1(i, s):
                act.wait_ge(c_var, pair(i, s) + 1)
                nc.scalar.activation(std[:, s, :], mean_var[:, s, 1:2], ACT.Sqrt, bias=eps_t[:, :]
                                     ).then_inc(c_std, 1)

            def c_norm1(i, s):
                act.wait_ge(c_shift, pair(i, s) + 1)
                nc.scalar.activation(y_t[:, s, :], h0_t[:, s, :], ACT.Identity, bias=shift[:, s, :],
                                     scale=rstd[:, s, :]).then_inc(c_y, 1)

            def c_norm2(i, s):
                act.wait_ge(c_var2, pair(i, s) + 1)
                nc.scalar.activation(std2[:, s, :], mean_var2[:, s, 1:2], ACT.Sqrt, bias=eps_t[:, :]
                                     ).then_inc(c_std2, 1)
                act.wait_ge(c_shift2, pair(i, s) + 1)
                nc.scalar.activation(h2_t[:, s, :], x2_t[:, s, :], ACT.Relu, bias=shift2[:, s, :],
                                     scale=rstd2[:, s, :]).then_inc(c_h2, 1)

            def c_copy_T(i, s):
                act.wait_ge(c_T, pair(i, s) + 1)
                nc.scalar.activation(h2T_t[:, 0, :], psum[:, s, :], ACT.Copy).then_inc(c_Tc, 1)

            def c_copy_up(i, s):
                t = pair(i, s)
                act.wait_ge(c_up, t + 1)
                act.wait_ge(c_up_free, t + 1)
                nc.scalar.activation(up_t[:, s, :], psum[:, 2 + s, :], ACT.Copy).then_inc(c_upc, 1)

            def c_both(i, s, i1, s1, before=None):
                if before:
                    c_copy_up(*before)
                c_std1(i1, s1)
                c_norm2(i, s)
                c_norm1(i1, s1)
                c_copy_T(i, s)

            c_std1(0, 0)
            c_norm1(0, 0)
            c_both(0, 0, 0, 1)
            c_both(0, 1, 1, 0, before=(0, 0))
            with act.Fori(1, NT // 2) as i:
                c_both(i, 0, i, 1, before=(i - 1, 1))
                c_both(i, 1, i + 1, 0, before=(i, 0))
            c_copy_up(NT // 2 - 1, 1)
            c_norm2(NT // 2, 0)
            c_copy_T(NT // 2, 0)
            c_copy_up(NT // 2, 0)
            barrier(act, 4)

            act.sem_inc(dm.act[2], 1)
            act.sem_inc(dx.act[2], 1)
            act.sem_inc(dm.sum_copied, 1)
            act.sem_inc(dx.sum_copied, 1)
            act.sem_inc(dm.T_copied, 1)
            act.sem_inc(dx.T_copied, 1)
            act.sem_inc(dm.staged, dm.bufs)
            act.sem_inc(dx.staged, dx.bufs)
            scales = [BASIS ** -0.5, SILU_2MOM * HID ** -0.5, SILU_2MOM * HID ** -0.5]

            def silu(x_, n, k, s):
                act.wait_ge(x_.layer[n], k + 1)
                to = (h1[:, 0, :], h2[:, 0, :], h3[:, s, :])[n]
                nc.scalar.activation(to, psum[:, 0, 0:HALF], ACT.Silu, scale=scales[n]).then_inc(x_.act[n], 1)

            def copy_sum(x_, k):
                act.wait_ge(x_.tile, k * TJ + TJ + RING)
                act.wait_ge(x_.T, k + 1)
                nc.scalar.activation(sum_sb[:, 0, :], flat[:, 3 * D:5 * D], ACT.Copy).then_inc(x_.sum_copied, 1)

            def copy_T(x_, k):
                act.wait_ge(x_.T, k + 2)
                act.wait_ge(x_.o, k + 1)
                nc.scalar.activation(sumT_sb[:, 0, :], flat[:, 5 * D:7 * D], ACT.Copy).then_inc(x_.T_copied, 1)

            def copy_o(x_, k, s):
                act.wait_ge(x_.o, k + 2)
                act.wait_ge(x_.stage_free, k + 1)
                nc.scalar.activation(o_sb[:, s, 0:MUL], psum[:, 7, 0:MUL], ACT.Copy)
                nc.scalar.activation(o_sb[:, s, MUL:4 * MUL].rearrange("p (v m) -> p m v", m=3),
                                     psum[:, 7, MUL:4 * MUL].rearrange("p (m v) -> p m v", m=3),
                                     ACT.Copy).then_inc(x_.staged, 1)

            def parts(x_, g, k, j):
                T, b = k * TJ + j, j
                act.wait_ge(x_.prod, T + 1 + TJ * x_.slots)
                for c in range(3):
                    nc.scalar.activation(prod[:, b, (2 + 2 * c) * MUL:(3 + 2 * c) * MUL], u_t[:, b, :], ACT.Copy,
                                         scale=attr[:, 0, bass.ds((g * TJ + j) * 4 + 1 + c, 1)]
                                         ).then_inc(x_.p2, 1)
                act.wait_ge(x_.p2, T * 3 + 3)
                act.wait_ge(x_.tile, T + 1)
                nc.scalar.activation(hi[:, b, :], prod[:, b, :], ACT.Copy).then_inc(x_.hi, 1)

            def d_step(k, s, known=None):
                def has(step):
                    return known is None or 0 <= known + step < NG
                if has(0):
                    parts(dm, k, k, 0)
                if has(1):
                    silu(dm, 2, k + 1, 1 - s % 2)
                if has(0):
                    parts(dm, k, k, 1)
                if has(-1):
                    copy_sum(dm, k - 1)
                if has(0):
                    parts(dm, k, k, 2)
                if has(2):
                    silu(dm, 0, k + 2, s % 2)
                if has(-2):
                    copy_o(dm, k - 2, s % 2)
                if has(0):
                    parts(dm, k, k, 3)
                if has(2):
                    silu(dm, 1, k + 2, s % 2)
                if has(-1):
                    copy_T(dm, k - 1)

            for n in range(3):
                silu(dm, n, 0, 0)
            for n in range(2):
                silu(dm, n, 1, 1)
            for k in range(D_SLOTS):
                d_step(k, k, known=k)
            with act.Fori(1, NG // D_SLOTS - 1) as i:
                for s in range(D_SLOTS):
                    d_step(i * D_SLOTS + s, s)
            for k in range(NG - D_SLOTS, NG + 1):
                d_step(k, k % D_SLOTS, known=k)
            copy_o(dm, NG - 1, 1)
            barrier(act, 5)

            def general_d(x_, g, w, k):
                for n in range(3):
                    silu(x_, n, k, 0)
                for j in range(TJ):
                    parts(x_, g, k, j)
                copy_sum(x_, k)
                copy_T(x_, k)
                copy_o(x_, k, 0)
            general_pass(act, dx, general_d)

        @block.vector
        def _(dve):
            setup = Chain(dve, s_setup)
            nc.vector.memset(big[:, 0:AW], 0.0).then_inc(s_zeroed, 1)
            dve.wait_ge(s_dst, 32)
            rows2 = dst_r_i[:, :].rearrange("p (c e) -> p c e", c=2)
            setup.link(nc.vector.tensor_reduce(least[:, :], rows2, AX.X, ALU.min))
            setup.link(nc.vector.tensor_reduce(more[:, :], rows2, AX.X, ALU.max))
            setup.link(nc.vector.tensor_tensor(more[:, :], more[:, :], least[:, :], ALU.subtract))
            nc.vector.tensor_scalar(more[:, :], more[:, :], int(math.log2(P)), None, ALU.arith_shift_right
                                    ).then_inc(s_meta_made, 1)
            dve.wait_ge(s_meta_in, 32)
            setup.link(nc.vector.memset(zero_f[:, :], 0.0))
            setup.link(nc.vector.tensor_copy(more_f[:, :], meta_row[0:1, MORE:MORE + NG]))
            setup.link(nc.vector.tensor_tensor_scan(prefix_f[:, :], more_f[:, :], zero_f[:, :], 0.0,
                                                    ALU.add, ALU.add))
            setup.link(nc.vector.tensor_copy(meta_row[0:1, 3 * NG:3 * NG + 1], prefix_f[0:1, NG - 1:NG]))
            setup.link(nc.vector.tensor_tensor(meta_row[0:1, BEFORE:BEFORE + NG], prefix_f[:, :], more_f[:, :],
                                               ALU.subtract))
            start_v = start_bc[:, :].unsqueeze(2).to_broadcast([P, NG, TJ])
            setup.link(nc.vector.tensor_tensor(rel[:, :].rearrange("p (g j) -> p g j", j=TJ),
                                               dst_c_i[:, :].rearrange("p (g j) -> p g j", j=TJ), start_v,
                                               ALU.subtract))
            full, part = divmod(N_EDGES, P)
            for p0 in range(part, P, 32):
                setup.link(nc.vector.memset(rel[p0:p0 + 32, full:full + 1], DEAD))
            setup.link(nc.vector.memset(rel[:, full + 1:], DEAD))
            dve.wait_ge(s_w, 8 * 16)
            setup.link(nc.vector.tensor_scalar(w_up[:, :, :], w_up[:, :, :], MUL ** -0.5, None, ALU.mult))
            dve.wait_ge(s_zero, 16 * (WINDOW_ROWS // P + 1))

            dve.sem_inc(a_res, 2)
            dve.sem_inc(a_kept, 2)

            def a_front(i, s):
                t = pair(i, s)
                chain = Chain(dve, a_chain, t * 2)
                dve.wait_ge(a_x_in[s], (i + 1) * 16)
                chain.link(nc.vector.bn_stats(stats[:, s, :], xt[:, s, :]))
                hold(dve)
                nc.vector.bn_aggr(mean_var[:, s, :], stats[:, s, :]).then_inc(a_var, 1)
                dve.wait_ge(a_std, t + 1)
                chain.link(nc.vector.reciprocal(rstd[:, s, :], std[:, s, :]))
                nc.vector.tensor_scalar(shift[:, s, :], mean_var[:, s, 0:1], rstd[:, s, :], -1.0,
                                        ALU.mult, ALU.mult).then_inc(a_shift, 1)

            def a_back(i, s):
                t = pair(i, s)
                dve.wait_ge(a_h, t + 1)
                dve.wait_ge(a_out_free, t + 1)
                nc.vector.tensor_tensor(res_t[:, s, :], xt[:, s, :], ht[:, s, :], ALU.add).then_inc(a_res, 1)
                dve.wait_ge(a_Tc, t + 1)
                nc.vector.tensor_copy(big[:, bass.ds(t * D, D)], h_t[:, s, :]).then_inc(a_kept, 1)

            a_front(0, 0)
            with dve.Fori(0, NT // 2) as i:
                a_front(i, 1)
                a_back(i, 0)
                a_front(i + 1, 0)
                a_back(i, 1)
            a_back(NT // 2, 0)
            barrier(dve, 1)

            def select(x_, rel_of, s):
                nc.vector.tensor_tensor(sel[:, s, :].rearrange("p (j n) -> p j n", j=TJ),
                                        iota_n[:, :].unsqueeze(1).to_broadcast([P, TJ, P]),
                                        rel_of.unsqueeze(2).to_broadcast([P, TJ, P]), ALU.is_equal
                                        ).then_inc(x_.sel, 1)

            def rel_main(g):
                return rel[:, bass.ds(g * TJ, TJ)]

            def rel_of_window(x_, g, w, k):
                nc.vector.tensor_scalar(rel_w[:, :], rel[:, bass.ds(g * TJ, TJ)], window_start[:, bass.ds(w, 1)],
                                        None, ALU.subtract).then_inc(x_.relw, 1)
                dve.wait_ge(x_.relw, k + 1)
                return rel_w[:, :]

            def b_lo(x_, s, k):
                for j in range(TJ):
                    dve.wait_ge(x_.hi, k * TJ + j + 1)
                    b = (s % x_.bufs) * TJ + j
                    nc.vector.tensor_tensor(lo_b[:, b, :], rows[s][:, j * D:(j + 1) * D],
                                            hi_b[:, b, :].bitcast(F32), ALU.subtract).then_inc(x_.lo, 1)

            dve.sem_inc(b_kept, 1)
            with dve.Fori(0, NT) as i:
                for s in range(B_SLOTS):
                    k = i * B_SLOTS + s
                    dve.wait_ge(bm.summed, k + 1)
                    select(bm, rel_main(k), s)
                    b_lo(bm, s, k)
                    if s == 2:
                        dve.wait_ge(b_self_mm, i + 1)
                        nc.vector.tensor_tensor(self_part[:, bass.ds(i * D, D)], psum[:, 4, :], bias_bc[:, :],
                                                ALU.add).then_inc(b_kept, 1)
            barrier(dve, 2)

            def general_b(x_, g, w, k):
                dve.wait_ge(x_.summed, k + 1)
                select(x_, rel_of_window(x_, g, w, k), 0)
                b_lo(x_, 0, k)
            general_pass(dve, bx, general_b)
            barrier(dve, 3)

            dve.sem_inc(c_x2, 2)
            IN_LINKS, OUT_LINKS = 5, 4

            def c_in_a(chain, i, s):
                t = pair(i, s)
                dve.wait_ge(c_in[s], (i + 1) * 32)
                chain.link(nc.vector.tensor_scalar(deg[:, s, :], acc_t[:, s, D:AW], 1.0, None, ALU.max))
                chain.link(nc.vector.reciprocal(rdeg[:, s, :], deg[:, s, :]))
                chain.link(nc.vector.scalar_tensor_tensor(
                    h0_t[:, s, :], acc_t[:, s, 0:D], rdeg[:, s, :], self_part[:, bass.ds(t * D, D)],
                    ALU.mult, ALU.add))
                chain.link(nc.vector.bn_stats(stats[:, s, :], h0_t[:, s, :]))
                hold(dve)
                nc.vector.bn_aggr(mean_var[:, s, :], stats[:, s, :]).then_inc(c_var, 1)

            def c_in_b(chain, i, s):
                dve.wait_ge(c_std, pair(i, s) + 1)
                chain.link(nc.vector.reciprocal(rstd[:, s, :], std[:, s, :]))
                nc.vector.tensor_scalar(shift[:, s, :], mean_var[:, s, 0:1], rstd[:, s, :], -1.0,
                                        ALU.mult, ALU.mult).then_inc(c_shift, 1)

            def c_out_c(chain, i, s):
                t = pair(i, s)
                y = y_t[:, s, :]
                dve.wait_ge(c_affine, t * 2 + 2)
                chain.link(nc.vector.tensor_scalar(neg_t[:, 0, :], y, 0.0, alpha_bc[:, :], ALU.min, ALU.mult))
                chain.link(nc.vector.scalar_tensor_tensor(y, y, 0.0, neg_t[:, 0, :], ALU.max, ALU.add))
                dve.wait_ge(c_x2_free, t + 1)
                dve.wait_ge(c_h2, t + 1)
                nc.vector.tensor_tensor(x2_t[:, s, :], y, res_c[:, s, :], ALU.add).then_inc(c_x2, 1)
                dve.wait_ge(c_x2, t + 3)
                chain.link(nc.vector.bn_stats(stats2[:, s, :], x2_t[:, s, :]))
                hold(dve)
                nc.vector.bn_aggr(mean_var2[:, s, :], stats2[:, s, :]).then_inc(c_var2, 1)

            def c_out_d(chain, i, s):
                dve.wait_ge(c_std2, pair(i, s) + 1)
                chain.link(nc.vector.reciprocal(rstd2[:, s, :], std2[:, s, :]))
                nc.vector.tensor_scalar(shift2[:, s, :], mean_var2[:, s, 0:1], rstd2[:, s, :], -1.0,
                                        ALU.mult, ALU.mult).then_inc(c_shift2, 1)

            def c_both(i, s, i1, s1):
                chain = Chain(dve, c_chain, pair(i, s) * (IN_LINKS + OUT_LINKS) + IN_LINKS)
                c_in_a(chain, i1, s1)
                c_out_c(chain, i, s)
                c_out_d(chain, i, s)
                c_in_b(chain, i1, s1)
                assert chain.n == IN_LINKS + OUT_LINKS

            chain = Chain(dve, c_chain)
            c_in_a(chain, 0, 0)
            c_in_b(chain, 0, 0)
            assert chain.n == IN_LINKS
            with dve.Fori(0, NT // 2) as i:
                c_both(i, 0, i, 1)
                c_both(i, 1, i + 1, 0)
            chain = Chain(dve, c_chain, (NT - 1) * (IN_LINKS + OUT_LINKS) + IN_LINKS)
            c_out_c(chain, NT // 2, 0)
            c_out_d(chain, NT // 2, 0)
            barrier(dve, 4)

            dve.wait_ge(s_dw, 7 * 16)
            silu_scale = SILU_2MOM * HID ** -0.5
            nc.vector.tensor_scalar(w4_sb[:, 0, 0:3 * MUL], w4_sb[:, 0, 0:3 * MUL], silu_scale, None, ALU.mult)
            nc.vector.tensor_scalar(w4_sb[:, 0, 3 * MUL:], w4_sb[:, 0, 3 * MUL:], silu_scale / math.sqrt(3.0),
                                    None, ALU.mult)
            nc.vector.tensor_scalar(wout_sb[:, :, :], wout_sb[:, :, :], (2 * MUL) ** -0.5 / AVG_NEIGHBORS,
                                    None, ALU.mult).then_inc(s_dw_scaled, 1)
            for x_ in (dm, dx):
                dve.sem_inc(x_.prod, TJ * x_.slots)
                dve.sem_inc(x_.lo_v, RING)

            def products(x_, g, s, k, j):
                T, b = k * TJ + j, j
                m, w = prod[:, b, :], psum[:, 1 + j % 2, :]
                row = rows[s][:, j * D:(j + 1) * D]
                s0, s1 = row[:, 0:MUL], row[:, MUL:]
                y = [attr[:, 0, bass.ds((g * TJ + j) * 4 + c, 1)] for c in range(4)]
                q = q_t[:, b, :]
                dve.wait_ge(x_.lo_v, T + 1)
                dve.wait_ge(x_.lo_p, T + 1)
                nc.vector.tensor_scalar(q[:, 0:MUL], s1[:, 0:MUL], y[1], None, ALU.mult).then_inc(x_.q, 1)
                dve.wait_ge(x_.weights, T + 1)
                nc.vector.scalar_tensor_tensor(
                    m[:, 2 * MUL:].rearrange("p (m c) -> p m c", m=3)[:, :, MUL:],
                    w[:, 2 * MUL:3 * MUL].unsqueeze(1).to_broadcast([P, 3, MUL]), y[0],
                    s1.rearrange("p (m c) -> p m c", m=3), ALU.mult, ALU.mult)
                dve.wait_ge(x_.q, T * 3 + 1)
                nc.vector.scalar_tensor_tensor(q[:, MUL:2 * MUL], s1[:, MUL:2 * MUL], y[2], q[:, 0:MUL],
                                               ALU.mult, ALU.add).then_inc(x_.q, 1)
                nc.vector.scalar_tensor_tensor(m[:, 0:MUL], w[:, 0:MUL], y[0], s0, ALU.mult, ALU.mult)
                dve.wait_ge(x_.q, T * 3 + 2)
                nc.vector.scalar_tensor_tensor(q[:, 2 * MUL:], s1[:, 2 * MUL:], y[3], q[:, MUL:2 * MUL],
                                               ALU.mult, ALU.add).then_inc(x_.q, 1)
                nc.vector.tensor_tensor(u_t[:, b, :], w[:, MUL:2 * MUL], s0, ALU.mult)
                dve.wait_ge(x_.q, T * 3 + 3)
                nc.vector.tensor_tensor(m[:, MUL:2 * MUL], w[:, 3 * MUL:], q[:, 2 * MUL:], ALU.mult
                                        ).then_inc(x_.prod, 1)

            def lo_tile(x_, k, j):
                T, b = k * TJ + j, j
                dve.wait_ge(x_.hi, T + 1)
                nc.vector.tensor_tensor(lo[:, b, 0:V_COLS], prod[:, b, 0:V_COLS], hi[:, b, 0:V_COLS].bitcast(F32),
                                        ALU.subtract).then_inc(x_.lo_v, 1)

            def d_step(i, s, first=False):
                k = i * D_SLOTS + s
                select(dm, rel_main(k), s)
                dve.wait_ge(dm.rows_in[s], (i + 1) * 16 * TJ)
                for j in range(TJ):
                    products(dm, k, s, k, j)
                    if j >= 2:
                        lo_tile(dm, k, j - 2)
                    elif not first:
                        lo_tile(dm, k - 1, j + 2)

            for s in range(D_SLOTS):
                d_step(0, s, first=(s == 0))
            with dve.Fori(1, NG // D_SLOTS) as i:
                for s in range(D_SLOTS):
                    d_step(i, s)
            lo_tile(dm, NG - 1, 2)
            lo_tile(dm, NG - 1, 3)
            barrier(dve, 5)

            def general_d(x_, g, w, k):
                rel_of = rel_of_window(x_, g, w, k)
                dve.wait_ge(x_.tile, k * TJ + RING)
                select(x_, rel_of, 0)
                dve.wait_ge(x_.rows_in[0], (k + 1) * 16 * TJ)
                for j in range(TJ):
                    products(x_, g, 0, k, j)
                    lo_tile(x_, k, j)
            general_pass(dve, dx, general_d)

        @block.tensor
        def _(pe):
            pe.wait_ge(s_const, 1)
            pe.wait_ge(s_w, 8 * 16)

            def a_step(i, s):
                t = pair(i, s)
                pe.wait_ge(a_h, t + 1)
                for c in range(KC):
                    last = nc.tensor.transpose(psum[:, s, c * P:(c + 1) * P], ht[:, s, c * P:(c + 1) * P],
                                               ident[:, :])
                last.then_inc(a_T, 1)
                pe.wait_ge(a_Tc, t + 1)
                pe.wait_ge(a_hn, t + 1)
                for c in range(KC):
                    last = nc.tensor.matmul(psum[:, 2 + s, :], h_t[:, s, c * P:(c + 1) * P], wn_sb[:, c, :],
                                            start=(c == 0), stop=(c == KC - 1))
                last.then_inc(a_mm, 1)

            with pe.Fori(0, NT // 2) as i:
                for s in range(2):
                    a_step(i, s)
            a_step(NT // 2, 0)
            barrier(pe, 1)

            pe.sem_inc(bm.summed, bm.slots)
            pe.sem_inc(bx.summed, bx.slots)

            def b_step(x_, i, s, s2, k):
                pe.wait_ge(x_.sel, k + 1)
                pe.wait_ge(x_.staged, k + 1)
                for j in range(TJ):
                    sel_j = sel[:, s, j * P:(j + 1) * P]
                    pe.wait_ge(x_.lo, k * TJ + j + 1)
                    for part in (hi_b, lo_b):
                        nc.tensor.matmul(psum[:, 2 * s2, :], sel_j, part[:, s2 * TJ + j, :],
                                         start=(j == 0 and part is hi_b), stop=(j == TJ - 1 and part is lo_b))
                    last = nc.tensor.matmul(psum[:, 2 * s2 + 1, 0:2], sel_j, ones[:, :],
                                            start=(j == 0), stop=(j == TJ - 1))
                last.then_inc(x_.summed, 1)

            def self_product(i):
                pe.wait_ge(b_hT, i + 1)
                for c in range(KC):
                    last = nc.tensor.matmul(psum[:, 4, :], hT_b[:, 0, c * P:(c + 1) * P], ws_sb[:, c, :],
                                            start=(c == 0), stop=(c == KC - 1))
                last.then_inc(b_self_mm, 1)

            with pe.Fori(0, NT) as i:
                for s in range(B_SLOTS):
                    b_step(bm, i, s, s % 2, i * B_SLOTS + s)
                    if s == 1:
                        self_product(i)
            barrier(pe, 2)
            general_pass(pe, bx, lambda x_, g, w, k: b_step(x_, k, 0, 0, k))
            barrier(pe, 3)

            def c_step(i, s):
                t = pair(i, s)
                pe.wait_ge(c_h2, t + 3)
                h = h2_t[:, s, :]
                nc.tensor.transpose(psum[:, s, 0:P], h[:, 0:MUL], ident[:, :])
                for m in range(3):
                    last = nc.tensor.transpose(psum[:, s, (m + 1) * P:(m + 2) * P], h[:, MUL + m::3], ident[:, :])
                last.then_inc(c_T, 1)
                pe.wait_ge(c_Tc, t + 1)
                pe.wait_ge(c_upc, t + 1)
                for m in range(4):
                    last = nc.tensor.matmul(psum[:, 2 + s, m * MUL:(m + 1) * MUL], h2T_t[:, 0, m * P:(m + 1) * P],
                                            w_up[:, min(m, 1), :], start=True, stop=True)
                last.then_inc(c_up, 1)

            with pe.Fori(0, NT // 2) as i:
                for s in range(2):
                    c_step(i, s)
            c_step(NT // 2, 0)
            barrier(pe, 4)

            pe.wait_ge(s_dw_scaled, 1)
            pe.sem_inc(dm.tile, RING)
            pe.sem_inc(dx.tile, RING)
            pe.sem_inc(dm.T, 1)
            pe.sem_inc(dx.T, 1)
            pe.sem_inc(dm.o, 1)
            pe.sem_inc(dx.o, 1)

            def mlp(x_, n, i, s, k):
                if n == 0:
                    pe.wait_ge(x_.feat_in[s], (i + 1) * 16)
                    pe.wait_ge(x_.act[2], k + 1)
                    w, h = w1_sb[0:2 * BASIS, 0, :], feat_t[0:2 * BASIS, s, :]
                else:
                    pe.wait_ge(x_.act[n - 1], k + 1)
                    w, h = ((w2_sb[:, 0, :], h1[:, 0, :]), (w3_sb[:, 0, :], h2[:, 0, :]))[n - 1]
                nc.tensor.matmul(psum[:, 0, 0:HALF], w, h, start=True, stop=True).then_inc(x_.layer[n], 1)

            def edge_weights(x_, s, k, j):
                T = k * TJ + j
                if j == 0:
                    pe.wait_ge(x_.act[2], k + 2)
                pe.wait_ge(x_.prod, T - 1 + TJ * x_.slots)
                half, col = (j % 2) * HID, (j // 2) * P
                nc.tensor.matmul(psum[:, 1 + j % 2, :], h3[half:half + HID, s % x_.bufs, col:col + P],
                                 w4_sb[half:half + HID, 0, :], start=True, stop=True).then_inc(x_.weights, 1)

            def sum_tile(x_, s, k, j):
                T = k * TJ + j
                pe.wait_ge(x_.lo_v, T + 1 + RING)
                pe.wait_ge(x_.lo_p, T + 1 + RING)
                if j == 0:
                    pe.wait_ge(x_.sel, k + 1)
                    pe.wait_ge(x_.sum_copied, k + 1)
                for b in range(2):
                    for part in (hi, lo):
                        last = nc.tensor.matmul(psum[:, 3 + b, :], sel[:, s, j * P:(j + 1) * P],
                                                part[:, j, b * D:(b + 1) * D],
                                                start=(j == 0 and part is hi), stop=(j == TJ - 1 and part is lo))
                last.then_inc(x_.tile, 1)

            def transpose_sum(x_, k):
                pe.wait_ge(x_.sum_copied, k + 2)
                pe.wait_ge(x_.T_copied, k + 1)
                for c in range(8):
                    last = nc.tensor.transpose(psum[:, 5 + c // 4, (c % 4) * P:(c % 4 + 1) * P],
                                               sum_sb[:, 0, c * P:(c + 1) * P], ident[:, :])
                last.then_inc(x_.T, 1)

            def output_maps(x_, k):
                pe.wait_ge(x_.T_copied, k + 2)
                pe.wait_ge(x_.staged, k + x_.bufs)
                for m in range(4):
                    for c in range(2):
                        last = nc.tensor.matmul(psum[:, 7, m * MUL:(m + 1) * MUL],
                                                sumT_sb[:, 0, (2 * m + c) * P:(2 * m + c + 1) * P],
                                                wout_sb[:, 2 * min(m, 1) + c, :], start=(c == 0), stop=(c == 1))
                last.then_inc(x_.o, 1)

            def d_step(i, s, known=None, last=False):
                k = i * D_SLOTS + s
                old = known is None
                i1, s1 = (i, s + 1) if s + 1 < D_SLOTS else (i + 1, 0)
                in_range = old or known < NG
                for j in range(TJ):
                    if in_range:
                        edge_weights(dm, s, k, j)
                    if j < 3 and not last and in_range:
                        mlp(dm, j, i1, s1, k + 1)
                    if j == 0 and (old or known >= 2):
                        transpose_sum(dm, k - 2)
                    if old or known >= 1:
                        sum_tile(dm, (s - 1) % D_SLOTS, k - 1, j)
                    if j == 2 and (old or known >= 2):
                        output_maps(dm, k - 2)

            for n in range(3):
                mlp(dm, n, 0, 0, 0)
            for s in range(D_SLOTS):
                d_step(0, s, known=s)
            with pe.Fori(1, NG // D_SLOTS - 1) as i:
                for s in range(D_SLOTS):
                    d_step(i, s)
            for s in range(D_SLOTS):
                d_step(NG // D_SLOTS - 1, s, last=(s == D_SLOTS - 1))
            d_step(NG // D_SLOTS, 0, known=NG)
            transpose_sum(dm, NG - 1)
            output_maps(dm, NG - 1)
            barrier(pe, 5)

            def general_d(x_, g, w, k):
                for n in range(3):
                    mlp(x_, n, k, 0, k)
                for j in range(TJ):
                    edge_weights(x_, 0, k, j)
                    sum_tile(x_, 0, k, j)
                transpose_sum(x_, k)
                output_maps(x_, k)
            general_pass(pe, dx, general_d)


def kernel(x, src, dst, edge_attr_4, edge_attr_8, L0_gnn_W_self, L0_gnn_b_self, L0_gnn_W_neigh, L0_gnn_gamma,
           L0_gnn_beta, L0_gnn_alpha, L1_gnn_W_up0, L1_gnn_W_up1, L1_gnn_W_mlp1, L1_gnn_W_mlp2, L1_gnn_W_mlp3,
           L1_gnn_W_mlp4, L1_gnn_W_out0, L1_gnn_W_out1):
    import concourse.bacc as bacc
    from concourse.bass_utils import run_bass_kernel_spmd

    a = np.asarray
    n_pad = NG * GE - N_EDGES

    def edge_pad(v):
        return np.concatenate([a(v), np.repeat(a(v)[-1:], n_pad, axis=0)])

    def to_rows(v):
        return np.ascontiguousarray(np.broadcast_to(a(v).reshape(1, -1), (P, a(v).size)))

    def columns(v):
        return np.ascontiguousarray(v.reshape(NG, TJ, P, -1).transpose(2, 0, 1, 3).reshape(P, -1))

    def block_diagonal(w):
        w = a(w)
        both = np.zeros((2 * w.shape[0], 2 * w.shape[1]), w.dtype)
        both[:w.shape[0], :w.shape[1]] = w
        both[w.shape[0]:, w.shape[1]:] = w
        return both

    x_pad = np.zeros((NP, D), a(x).dtype)
    x_pad[:N_NODES] = a(x)
    src_p, dst_p = edge_pad(src), edge_pad(dst)
    ins = {
        "x": x_pad,
        "src_g": np.ascontiguousarray(src_p.reshape(NG, TJ, P).transpose(0, 2, 1)),
        "dst_rows": dst_p.reshape(GP, 2 * GE),
        "dst_cols": columns(dst_p),
        "attr_cols": columns(edge_pad(edge_attr_4)),
        "feat_g": np.ascontiguousarray(edge_pad(edge_attr_8).reshape(NG, 2, 2, P, BASIS).transpose(0, 2, 4, 1, 3)
                                       .reshape(NG, 2 * BASIS, HALF)),
        "w_self": a(L0_gnn_W_self), "w_neigh": a(L0_gnn_W_neigh),
        "b_self": to_rows(L0_gnn_b_self), "gamma": to_rows(L0_gnn_gamma), "beta": to_rows(L0_gnn_beta),
        "alpha": to_rows(L0_gnn_alpha),
        "w_up0": a(L1_gnn_W_up0), "w_up1": a(L1_gnn_W_up1),
        "w_mlp1": block_diagonal(L1_gnn_W_mlp1), "w_mlp2": block_diagonal(L1_gnn_W_mlp2),
        "w_mlp3": block_diagonal(L1_gnn_W_mlp3),
        "w_mlp4": np.concatenate([a(L1_gnn_W_mlp4)] * 2),
        "w_out0": a(L1_gnn_W_out0), "w_out1": a(L1_gnn_W_out1),
    }
    nc = bacc.Bacc("TRN2", target_bir_lowering=False, num_devices=1)
    aps = {name: nc.dram_tensor(f"in_{name}", v.shape, mybir.dt.from_np(v.dtype), kind="ExternalInput").ap()
           for name, v in ins.items()}
    out = nc.dram_tensor("out_0", (WINDOW_ROWS, D), F32, kind="ExternalOutput").ap()
    gnn_kernel(nc, *aps.values(), out)
    r = run_bass_kernel_spmd(nc, [{f"in_{name}": v for name, v in ins.items()}], core_ids=[0])
    return r.results[0]["out_0"][:N_NODES]
```

```python
import math
from contextlib import ExitStack

import numpy as np
import concourse.bass as bass
from concourse import mybir

F32 = mybir.dt.float32
F32R = mybir.dt.float32r
I32 = mybir.dt.int32
ALU = mybir.AluOpType
ACT = mybir.ActivationFunctionType
AX = mybir.AxisListType

P = 128
N_NODES, D = 6250, 512
N_EDGES = 100000
KC = D // P
NT = -(-N_NODES // P)
NP = NT * P
WINDOW_ROWS = NP + P
TJ = 4
GE = TJ * P
NG = -(-N_EDGES // GE)
MUL = 128
HID = 64
BASIS = 8
HALF = GE // 2
LN_EPS = 1e-5
SILU_2MOM = 1.679177
AVG_NEIGHBORS = 10.0
AW = D + 1
NW = NG // 2
B_SLOTS, B_LAG = 4, 5
D_SLOTS, D_LAG = 4, 7
RING = TJ
MSG_AHEAD = 2
DEAD = -1.0e6
assert NG % B_SLOTS == 0 and NG == NT * B_SLOTS and NG % D_SLOTS == 0 and NG % 2 == 0 and NT % 2 == 1
GP = NG // 2


def gnn_kernel(nc, x, src_g, dst_rows, dst_cols, attr_cols, feat_g, w_self, w_neigh, b_self, gamma, beta,
               alpha, w_up0, w_up1, w_mlp1, w_mlp2, w_mlp3, w_mlp4, w_out0, w_out1, out):
    table0 = nc.dram_tensor("table0", (NP, D), F32, kind="Internal").ap()
    table1 = nc.dram_tensor("table1", (NP, D), F32, kind="Internal").ap()
    resid = nc.dram_tensor("resid", (NP, D), F32, kind="Internal").ap()
    acc0 = nc.dram_tensor("acc0", (WINDOW_ROWS, AW), F32, kind="Internal").ap()
    meta = nc.dram_tensor("meta", (2, NG), I32, kind="Internal").ap()

    with ExitStack() as ctx:
        def sb(name, shape, dt=F32):
            return ctx.enter_context(nc.sbuf_tensor(name, shape, dt))

        def sem(name):
            return ctx.enter_context(nc.semaphore(name))

        def carve(arena, sizes):
            views, at = [], 0
            for shape in sizes:
                n = math.prod(shape)
                v = arena[:, at:at + n]
                if len(shape) == 2:
                    v = v.rearrange("p (a b) -> p a b", a=shape[0])
                if len(shape) == 3:
                    v = v.rearrange("p (a b c) -> p a b c", a=shape[0], b=shape[1])
                views.append(v)
                at += n
            assert at <= arena.shape[1], (at, arena.shape)
            return views

        big = sb("big", [P, NT * D])
        sel = sb("sel", [P, 4, TJ * P], F32R)
        hi = sb("hi", [P, RING, 8 * MUL], F32R)
        lo = sb("lo", [P, RING, 8 * MUL], F32R)
        ones = sb("ones", [P, 2], F32R)
        work = sb("work", [P, KC * D + D + 2 * AW + 2 * TJ * D])
        self_part = big
        bias_bc, gamma_bc, beta_bc = sb("bias_bc", [P, D]), sb("gamma_bc", [P, D]), sb("beta_bc", [P, D])
        alpha_bc = sb("alpha_bc", [P, 1])
        eps_t = sb("eps_t", [P, 1])
        ident = sb("ident", [P, P])
        iota_n = sb("iota_n", [P, P])
        window_start = sb("window_start", [P, NT])
        rel = sb("rel", [P, NG * TJ])
        rel_w = sb("rel_w", [P, TJ])
        src_idx = [sb(f"src_idx{s}", [P, TJ], I32) for s in range(B_SLOTS)]
        meta_row = sb("meta_row", [1, 4 * NG], I32)
        START, MORE, BEFORE, TOTAL = 0, NG, 2 * NG, 3 * NG
        FIRST, SPAN = 3 * NG + 1, 3 * NG + 2
        stats = sb("stats", [P, 2, 6])
        mean_var = sb("mean_var", [P, 2, 2])
        std = sb("std", [P, 2, 1])
        rstd = sb("rstd", [P, 2, 1])
        shift = sb("shift", [P, 2, 1])
        stats2 = sb("stats2", [P, 2, 6])
        mean_var2 = sb("mean_var2", [P, 2, 2])
        std2 = sb("std2", [P, 2, 1])
        rstd2 = sb("rstd2", [P, 2, 1])
        shift2 = sb("shift2", [P, 2, 1])
        deg = sb("deg", [P, 2, 1])
        rdeg = sb("rdeg", [P, 2, 1])
        w_up = sb("w_up", [P, 2, MUL])

        ws_sb, wn_sb, xt, ht, h_t = carve(work, [(KC, D), (KC, D), (2, D), (2, D), (2, D)])
        _, hT_b, stage_b, rows_in_work = carve(work, [(KC, D), (1, D), (2, AW), (2, TJ * D)])
        rows_alone = sb("rows_alone", [P, B_SLOTS - 2, TJ * D])
        hn_t, res_t, dst_r, dst_c, start_c = carve(
            rows_alone[:, :, :].rearrange("p a b -> p (a b)"), [(2, D), (2, D), (2 * GE,), (NG * TJ,), (NG,)])
        dst_r_i, dst_c_i, start_bc = dst_r[0:GP, :].bitcast(I32), dst_c.bitcast(I32), start_c.bitcast(I32)
        up_t = rows_alone[:, 0, 0:2 * D].rearrange("p (a b) -> p a b", a=2)
        zero = lo[:, 0, 0:AW].bitcast(F32)
        rows = [rows_alone[:, 0, :], rows_alone[:, 1, :], rows_in_work[:, 0, :], rows_in_work[:, 1, :]]
        hi_b = hi[:, :, :].rearrange("p a (b n) -> p (a b) n", b=2)
        lo_b = lo[:, :, :].rearrange("p a (b n) -> p (a b) n", b=2)
        acc_t, res_c, h0_t, y_t, neg_t, x2_t, h2_t, h2T_t = carve(
            work, [(2, AW), (2, D), (2, D), (2, D), (1, D), (2, D), (2, D), (2, D)])
        (prod_u, q_t, feat_t, h1, h2, h3, sum_sb, sumT_sb, o_sb, attr, w1_sb, w2_sb, w3_sb, w4_sb,
         wout_sb) = carve(
            big, [(RING, 9 * MUL), (RING, 3 * MUL), (D_SLOTS, HALF),
                  (1, HALF), (1, HALF), (2, HALF), (1, 8 * MUL), (1, 8 * MUL), (2, 4 * MUL),
                  (1, NG * TJ * 4), (1, P), (1, P), (1, P), (1, D), (4, MUL)])
        prod = prod_u[:, :, 0:8 * MUL]

        def u_of(b):
            return prod_u[:, b, 8 * MUL:]

        def p1_u(b):
            return prod_u[:, b, :].rearrange("p (c v) -> p c v", v=MUL)[:, 0::8, :]

        least_g = sb("least_g", [GP, 2], I32)
        least = sb("least", [GP, 2], I32)
        more = sb("more", [GP, 2], I32)
        more_f = sb("more_f", [1, NG])
        zero_f = sb("zero_f", [1, NG])
        prefix_f = sb("prefix_f", [1, NG])
        from_start, from_end = sb("from_start", [1, NG]), sb("from_end", [1, NG])
        bound_f = sb("bound_f", [1, 2])

        psum = ctx.enter_context(nc.psum_tensor("psum", [P, 8, D], F32))
        flat = psum[:, :, :].rearrange("p b n -> p (b n)")

        s_bar = sem("s_barrier")
        s_held = sem("s_waits_held")
        s_wn = sem("s_w_neigh_in")
        s_w = sem("s_weights_in")
        s_dst = sem("s_dst_rows_in")
        s_dst_cols = sem("s_dst_columns_in")
        s_const = sem("s_constants_made")
        s_pool_const = sem("s_pool_constants")
        s_meta_made = sem("s_meta_made")
        s_meta_out = sem("s_meta_out")
        s_meta_in = sem("s_meta_in")
        s_setup = sem("s_setup_chain")
        s_zero = sem("s_zero_rows")
        s_zeroed = sem("s_zero_tile")

        ENGINES = 5

        def barrier(eng, n):
            eng.drain().then_inc(s_bar, 1)
            eng.wait_ge(s_bar, ENGINES * n)

        def hold(eng):
            eng.sem_inc(s_held, 1)

        class Chain:
            def __init__(self, eng, s, base=0):
                self.eng, self.s, self.base, self.n = eng, s, base, 0

            def link(self, ins):
                self.n += 1
                ins.then_inc(self.s, 1)
                self.eng.wait_ge(self.s, self.base + self.n)

        def rounds(eng, step, last):
            peel = 5
            for n in range(peel):
                step(n, n % 2, n // 2)
            with eng.Fori(peel // 2, NT // 2) as r:
                step(2 * r + 1, 1, r)
                step(2 * r + 2, 0, r + 1)
            for n in range(NT, last):
                step(n, n % 2, n // 2)

        def has(n, back=0, least=0):
            return not isinstance(n, int) or (0 <= n - back < NT and n >= least)

        a_x_in = [sem(f"a_x_in{s}") for s in range(2)]
        a_chain = sem("a_vector_chain")
        a_var = sem("a_variance")
        a_std = sem("a_std")
        a_shift = sem("a_shift")
        a_h = sem("a_h_ready")
        a_T = sem("a_h_transposed")
        a_Tc = sem("a_h_transposed_copied")
        a_mm = sem("a_products")
        a_hn = sem("a_neigh_copied")
        a_kept = sem("a_transposed_kept")
        a_res = sem("a_resid_made")
        a_res_out = [sem(f"a_resid_out{s}") for s in range(2)]
        a_hn_out = [sem(f"a_table_out{s}") for s in range(2)]

        class EdgeSemsB:
            def __init__(self, name, slots):
                self.slots = slots
                self.idx_in = [sem(f"{name}_idx_in{s}") for s in range(slots)]
                self.rows_in = [sem(f"{name}_rows_in{s}") for s in range(slots)]
                self.sel = sem(f"{name}_selection_made")
                self.hi = sem(f"{name}_hi")
                self.lo = sem(f"{name}_lo")
                self.relw = sem(f"{name}_rel_window")
                self.bufs = min(2, slots)
                self.summed = sem(f"{name}_summed")
                self.staged = sem(f"{name}_staged")
                self.stage_free = sem(f"{name}_stage_free")
                self.added = sem(f"{name}_added")

        bm = EdgeSemsB("b", B_SLOTS)
        bx = EdgeSemsB("bx", 1)
        b_hT = sem("b_hT_taken")
        b_self_mm = sem("b_self_product")
        b_kept = sem("b_self_kept")

        c_acc_in = [sem(f"c_acc_in{s}") for s in range(2)]
        c_res_in = [sem(f"c_resid_in{s}") for s in range(2)]
        c_chain_in, c_chain_out = sem("c_vector_chain_in"), sem("c_vector_chain_out")
        c_var, c_std, c_shift, c_y = sem("c_var"), sem("c_std"), sem("c_shift"), sem("c_y")
        c_affine = sem("c_affine")
        c_var2, c_std2, c_shift2 = sem("c_var2"), sem("c_std2"), sem("c_shift2")
        c_x2, c_h2 = sem("c_x2_made"), sem("c_h2_made")
        c_T, c_Tc, c_up = sem("c_h2_transposed"), sem("c_h2_transposed_copied"), sem("c_up_products")
        c_upc = sem("c_up_copied")
        c_x2_out = [sem(f"c_x2_out{s}") for s in range(2)]
        c_up_out = [sem(f"c_table_out{s}") for s in range(2)]

        class EdgeSemsD:
            def __init__(self, name, slots):
                self.slots = slots
                self.bufs = min(2, slots)
                self.feat_in = [sem(f"{name}_feat_in{s}") for s in range(slots)]
                self.idx_in = [sem(f"{name}_idx_in{s}") for s in range(slots)]
                self.rows_in = [sem(f"{name}_rows_in{s}") for s in range(slots)]
                self.relw = sem(f"{name}_rel_window")
                self.sel = sem(f"{name}_selection_made")
                self.layer = [sem(f"{name}_layer{n}") for n in range(3)]
                self.act = [sem(f"{name}_layer{n}_silu") for n in range(3)]
                self.weights = sem(f"{name}_edge_weights")
                self.q = sem(f"{name}_q_chain")
                self.prod = sem(f"{name}_products")
                self.p2 = sem(f"{name}_p2_chain")
                self.hi = sem(f"{name}_hi")
                self.lo_v = sem(f"{name}_lo_vector")
                self.lo_p = sem(f"{name}_lo_gpsimd")
                self.tile = sem(f"{name}_tile_summed")
                self.sum_copied = sem(f"{name}_sum_copied")
                self.T = sem(f"{name}_sum_transposed")
                self.T_copied = sem(f"{name}_sum_transposed_copied")
                self.o = sem(f"{name}_output_maps")
                self.staged = sem(f"{name}_staged")
                self.stage_free = sem(f"{name}_stage_free")
                self.added = sem(f"{name}_added")

        dm = EdgeSemsD("d", D_SLOTS)
        dx = EdgeSemsD("dx", 1)
        s_dw = sem("d_weights_in")
        s_attr = sem("d_edge_attributes_in")
        s_dw_scaled = sem("d_weights_scaled")

        def general_pass(eng, x, step):
            any_more = eng.value_load(meta_row[0:1, TOTAL:TOTAL + 1], min_val=0, max_val=NG * NT)
            with eng.If(any_more > 0):
                first = eng.value_load(meta_row[0:1, FIRST:FIRST + 1], min_val=0, max_val=NG - 1)
                span = eng.value_load(meta_row[0:1, SPAN:SPAN + 1], min_val=1, max_val=NG)
                with eng.Fori(0, span) as n:
                    g = nc.s_assert_within(first + n, 0, NG - 1)
                    n_more = eng.value_load(meta_row[0:1, bass.ds(g + MORE, 1)], min_val=0, max_val=NT - 1)
                    before = eng.value_load(meta_row[0:1, bass.ds(g + BEFORE, 1)], min_val=0, max_val=NG * NT)
                    with eng.If(n_more > 0):
                        with eng.Fori(0, n_more) as w:
                            step(x, g, w + 1, before + w)
                    eng.nop()
            eng.nop()

        block = ctx.enter_context(nc.Block())

        @block.sync
        def _(sp):
            sp.dma_start(dst_r_i[:, :], dst_rows).then_inc(s_dst, 16)

            def move_a(n, s, r):
                if has(n, 2):
                    sp.wait_ge(a_res, n - 1)
                if has(n):
                    sp.dma_start(xt[:, s, :], x[bass.ds(n * P, P), :]).then_inc(a_x_in[s], 16)
                if has(n, 2):
                    sp.dma_start(resid[bass.ds((n - 2) * P, P), :], res_t[:, s, :]).then_inc(a_res_out[s], 16)
                if has(n, 4):
                    sp.wait_ge(a_hn, n - 3)
                    sp.dma_start(table0[bass.ds((n - 4) * P, P), :], hn_t[:, s, :]).then_inc(a_hn_out[s], 16)
                if isinstance(n, int) and n == 1:
                    sp.dma_start(wn_sb, w_neigh.rearrange("(c p) n -> p c n", p=P)).then_inc(s_wn, 16)
                    sp.dma_start(dst_c_i[:, :], dst_cols).then_inc(s_dst_cols, 16)
                    load_first()
                if isinstance(n, int) and n == 3:
                    load_rest()

            def load_first():
                sp.wait_ge(s_meta_made, 1)
                sp.dma_start(meta[0, :].rearrange("(p c) -> p c", c=2), least[:, :]).then_inc(s_meta_out, 16)
                sp.dma_start(meta[1, :].rearrange("(p c) -> p c", c=2), more[:, :]).then_inc(s_meta_out, 16)

            def load_rest():
                sp.dma_start(bias_bc[:, :], b_self).then_inc(s_w, 16)
                sp.dma_start(gamma_bc[:, :], gamma).then_inc(s_w, 16)
                sp.dma_start(beta_bc[:, :], beta).then_inc(s_w, 16)
                sp.dma_start(alpha_bc[:, :], alpha).then_inc(s_w, 16)
                sp.dma_start(w_up[:, 0, :], w_up0).then_inc(s_w, 16)
                sp.dma_start(w_up[:, 1, :], w_up1).then_inc(s_w, 16)
                sp.dma_start(ws_sb, w_self.rearrange("(c p) n -> p c n", p=P)).then_inc(s_w, 16)
                sp.wait_ge(s_meta_out, 32)
                sp.dma_start(meta_row[0:1, 0:2 * NG], meta.rearrange("(a r) g -> a (r g)", a=1)
                             ).then_inc(s_meta_in, 16)
                sp.dma_start(start_bc[:, :], meta[0, :].partition_broadcast(P)).then_inc(s_meta_in, 16)

            def landed(out_sems):
                sp.wait_ge(out_sems[0], (NT + 1) // 2 * 16)
                sp.wait_ge(out_sems[1], NT // 2 * 16)

            rounds(sp, move_a, NT + 4)
            landed(a_res_out)
            landed(a_hn_out)
            barrier(sp, 1)

            def idx_b(x_, g, i, s, k):
                sp.wait_ge(x_.hi, k * TJ + 1)
                sp.dma_start(src_idx[s][:, :], src_g[bass.ds(g, 1), :, :].rearrange("a p j -> (a p) j")
                             ).then_inc(x_.idx_in[s], 16)

            with sp.Fori(0, NG // B_SLOTS) as i:
                for s in range(B_SLOTS):
                    k = i * B_SLOTS + s
                    idx_b(bm, k, i, s, k)
            barrier(sp, 2)
            general_pass(sp, bx, lambda x_, g, w, k: idx_b(x_, g, k, 0, k))
            barrier(sp, 3)

            def move_c(n, s, r):
                if has(n):
                    if has(n, 2):
                        sp.wait_ge(c_var, n - 1)
                    sp.dma_start(acc_t[:, s, :], acc0[bass.ds(n * P, P), :]).then_inc(c_acc_in[s], 16)
                if has(n, 4):
                    sp.wait_ge(c_x2, n - 3)
                if has(n, 2):
                    sp.dma_start(res_c[:, s, :], resid[bass.ds((n - 2) * P, P), :]).then_inc(c_res_in[s], 16)
                if has(n, 4):
                    sp.dma_start(out[bass.ds((n - 4) * P, P), :], x2_t[:, s, :]).then_inc(c_x2_out[s], 16)
                if has(n, 5):
                    sp.wait_ge(c_upc, n - 4)
                    sp.dma_start(table1[bass.ds((n - 5) * P, P), :], up_t[:, 1 - s, :]).then_inc(c_up_out[1 - s], 16)

            rounds(sp, move_c, NT + 5)
            landed(c_x2_out)
            landed(c_up_out)
            barrier(sp, 4)

            sp.dma_start(w1_sb[0:2 * BASIS, 0, :], w_mlp1).then_inc(s_dw, 16)
            sp.dma_start(w2_sb[:, 0, :], w_mlp2).then_inc(s_dw, 16)
            sp.dma_start(w3_sb[:, 0, :], w_mlp3).then_inc(s_dw, 16)
            sp.dma_start(w4_sb[:, 0, :], w_mlp4).then_inc(s_dw, 16)
            sp.dma_start(wout_sb[:, 0:2, :], w_out0.rearrange("(c p) n -> p c n", p=P)).then_inc(s_dw, 16)
            sp.dma_start(wout_sb[:, 2:4, :], w_out1.rearrange("(c p) n -> p c n", p=P)).then_inc(s_dw, 16)

            def inputs_d(x_, g, s, k):
                sp.wait_ge(x_.prod, k * TJ + 1)
                sp.dma_start(src_idx[s][:, :], src_g[bass.ds(g, 1), :, :].rearrange("a p j -> (a p) j")
                             ).then_inc(x_.idx_in[s], 16)
                sp.dma_start(feat_t[0:2 * BASIS, s, :], feat_g[bass.ds(g, 1), :, :].rearrange("a f e -> (a f) e")
                             ).then_inc(x_.feat_in[s], 16)

            for s in range(D_SLOTS):
                inputs_d(dm, s, s, s)
            sp.dma_start(attr[:, 0, :], attr_cols).then_inc(s_attr, 16)
            with sp.Fori(1, NG // D_SLOTS) as i:
                for s in range(D_SLOTS):
                    k = i * D_SLOTS + s
                    inputs_d(dm, k, s, k)
            barrier(sp, 5)
            general_pass(sp, dx, lambda x_, g, w, k: inputs_d(x_, g, 0, k))

        @block.gpsimd
        def _(pool):
            nc.gpsimd.memset(ident[:, :], 0.0).then_inc(s_pool_const, 1)
            nc.gpsimd.memset(ones[:, :].bitcast(F32), 1.0)
            nc.gpsimd.memset(eps_t[:, :], LN_EPS)
            nc.gpsimd.iota(iota_n[:, :], pattern=[[1, P]], base=0, channel_multiplier=0,
                           allow_small_or_imprecise_dtypes=True)
            nc.gpsimd.iota(window_start[:, :], pattern=[[P, NT]], base=0, channel_multiplier=0,
                           allow_small_or_imprecise_dtypes=True)
            nc.gpsimd.iota(from_start[:, :], pattern=[[1, NG]], base=1, channel_multiplier=0,
                           allow_small_or_imprecise_dtypes=True)
            nc.gpsimd.iota(from_end[:, :], pattern=[[-1, NG]], base=NG, channel_multiplier=0,
                           allow_small_or_imprecise_dtypes=True)
            pool.wait_ge(s_pool_const, 1)
            nc.gpsimd.affine_select(out=ident[:, :], in_=ident[:, :], compare_op=ALU.not_equal, fill=1.0,
                                    base=0, pattern=[[-1, P]], channel_multiplier=1).then_inc(s_const, 1)

            pool.wait_ge(s_zeroed, 1)
            with pool.Fori(0, NT) as t:
                pool.wait_ge(a_h, t + 1)
                hold(pool)
                pool.dma_start(acc0[bass.ds(t * P, P), :], zero).then_inc(s_zero, 16)
            pool.dma_start(acc0[NP:WINDOW_ROWS, :], zero).then_inc(s_zero, 16)
            pool.dma_start(out[NP:WINDOW_ROWS, :], zero[:, 0:D]).then_inc(s_zero, 16)
            pool.wait_ge(s_zero, 16 * (WINDOW_ROWS // P + 1))
            barrier(pool, 1)

            def gather_waits(x_, i, s, k, rows_free, per_step):
                pool.wait_ge(x_.idx_in[s], (i + 1) * 16)
                pool.wait_ge(rows_free, (k + 1) * per_step)
                hold(pool)

            def gather_tile(x_, table, s, j):
                nc.gpsimd.indirect_dma_start(
                    rows[s][:, j * D:(j + 1) * D], None, table,
                    bass.IndirectOffsetOnAxis(ap=src_idx[s][:, j:j + 1], axis=0)).then_inc(x_.rows_in[s], 16)

            def add_window(x_, target, stage, g, s, k, first=False):
                row = pool.value_load(meta_row[0:1, bass.ds(g + START, 1)], min_val=0, max_val=N_NODES - 1)
                pool.wait_ge(x_.staged, k + 1 + x_.bufs)
                if first:
                    hold(pool)
                else:
                    pool.wait_ge(x_.added, k * 16)
                    pool.sem_inc(x_.stage_free, 1)
                pool.dma_start(target[bass.ds(row, P), :], stage[:, s, :], accum_op=ALU.add
                               ).then_inc(x_.added, 16)

            def add_window_alone(x_, target, stage, g, w, k):
                row0 = pool.value_load(meta_row[0:1, bass.ds(g + START, 1)], min_val=0, max_val=N_NODES - 1)
                row = nc.s_assert_within(row0 + w * P, 0, WINDOW_ROWS - P)
                pool.wait_ge(x_.staged, k + 1 + x_.bufs)
                hold(pool)
                pool.dma_start(target[bass.ds(row, P), :], stage[:, 0, :], accum_op=ALU.add
                               ).then_inc(x_.added, 16)
                pool.wait_ge(x_.added, (k + 1) * 16)
                pool.sem_inc(x_.stage_free, 1)

            def steps_ahead(first_i, step):
                for k in range(first_i * 4):
                    step(k // 4, k % 4)
                with pool.Fori(first_i, NG // 4) as i:
                    for s in range(4):
                        step(i, s)

            pool.sem_inc(bm.stage_free, bm.bufs)
            pool.sem_inc(bx.stage_free, bx.bufs)

            def step_b(i, s):
                k = i * B_SLOTS + s
                known = isinstance(k, int)
                if s % 2 == 1 and not (known and k < B_LAG):
                    w = i * 2 + (s - B_LAG) // 2
                    add_window(bm, acc0, stage_b, k - B_LAG, (s - B_LAG) // 2 % 2, w, first=known and k == B_LAG)
                gather_waits(bm, i, s, k, bm.lo, TJ)
                for j in range(TJ):
                    gather_tile(bm, table0, s, j)

            steps_ahead(B_LAG // 4 + 1, step_b)
            for k in range(NW - B_LAG // 2, NW):
                add_window(bm, acc0, stage_b, 2 * k, k % 2, k)
            pool.wait_ge(bm.added, NW * 16)
            barrier(pool, 2)

            def general_b(x_, g, w, k):
                gather_waits(x_, k, 0, k, x_.lo, TJ)
                for j in range(TJ):
                    gather_tile(x_, table0, 0, j)
                add_window_alone(x_, acc0, stage_b, g, w, k)
            general_pass(pool, bx, general_b)
            barrier(pool, 3)

            def affine_c(n, s, r):
                pool.wait_ge(c_y, n + 1)
                nc.gpsimd.tensor_tensor(y_t[:, s, :], y_t[:, s, :], gamma_bc[:, :], ALU.mult).then_inc(c_affine, 1)
                pool.wait_ge(c_affine, n * 2 + 1)
                nc.gpsimd.tensor_tensor(y_t[:, s, :], y_t[:, s, :], beta_bc[:, :], ALU.add).then_inc(c_affine, 1)

            rounds(pool, affine_c, NT)
            barrier(pool, 4)

            pool.sem_inc(dm.stage_free, dm.bufs)
            pool.sem_inc(dx.stage_free, dx.bufs)
            pool.sem_inc(dm.lo_p, RING)
            pool.sem_inc(dx.lo_p, RING)

            def lo_tile(x_, k, j):
                T, b = k * TJ + j, j
                pool.wait_ge(x_.hi, T + 1)
                nc.gpsimd.tensor_tensor(lo[:, b, D:], prod[:, b, D:], hi[:, b, D:].bitcast(F32),
                                        ALU.subtract).then_inc(x_.lo_p, 1)

            def step_d(i, s):
                k = i * D_SLOTS + s
                known = isinstance(k, int)
                gather_waits(dm, i, s, k, dm.prod, TJ)
                for j in range(TJ):
                    gather_tile(dm, table1, s, j)
                    if not known or k >= MSG_AHEAD:
                        lo_tile(dm, k - MSG_AHEAD, j)
                if s % 2 == 1 and not (known and k < D_LAG):
                    w = i * 2 + (s - D_LAG) // 2
                    add_window(dm, out, o_sb, k - D_LAG, (s - D_LAG) // 2 % 2, w, first=known and k == D_LAG)

            steps_ahead(2, step_d)
            for k in range(NG, NG + D_LAG):
                if k - MSG_AHEAD < NG:
                    for j in range(TJ):
                        lo_tile(dm, k - MSG_AHEAD, j)
                if k % 2 == 1:
                    w = (k - D_LAG) // 2
                    add_window(dm, out, o_sb, 2 * w, w % 2, w)
            pool.wait_ge(dm.added, NW * 16)
            barrier(pool, 5)

            def general_d(x_, g, w, k):
                gather_waits(x_, k, 0, k, x_.prod, TJ)
                for j in range(TJ):
                    gather_tile(x_, table1, 0, j)
                for j in range(TJ):
                    lo_tile(x_, k, j)
                add_window_alone(x_, out, o_sb, g, w, k)
            general_pass(pool, dx, general_d)

        @block.scalar
        def _(act):
            act.wait_ge(s_const, 1)

            def a_step(n, s, r):
                if has(n):
                    act.wait_ge(a_var, n + 1)
                    nc.scalar.activation(std[:, s, :], mean_var[:, s, 1:2], ACT.Sqrt, bias=eps_t[:, :]
                                         ).then_inc(a_std, 1)
                    act.wait_ge(a_shift, n + 1)
                    if has(n, 2):
                        act.wait_ge(a_res, n - 1)
                    nc.scalar.activation(ht[:, s, :], xt[:, s, :], ACT.Relu, bias=shift[:, s, :],
                                         scale=rstd[:, s, :]).then_inc(a_h, 1)
                if has(n, 1):
                    act.wait_ge(a_T, n)
                    if has(n, 1, least=3):
                        act.wait_ge(a_kept, n - 2)
                    nc.scalar.activation(h_t[:, 1 - s, :], psum[:, 1 - s, :], ACT.Copy).then_inc(a_Tc, 1)
                if has(n, 2):
                    act.wait_ge(a_mm, n - 1)
                    if has(n, 2, least=4):
                        act.wait_ge(a_hn_out[s], (r - 1) * 16)
                    nc.scalar.activation(hn_t[:, s, :], psum[:, 2 + s, :], ACT.Copy).then_inc(a_hn, 1)

            rounds(act, a_step, NT + 2)
            barrier(act, 1)

            act.sem_inc(bm.staged, bm.bufs)
            act.sem_inc(bx.staged, bx.bufs)
            act.sem_inc(bm.hi, TJ * bm.slots)
            act.sem_inc(bx.hi, TJ * bx.slots)

            def b_hi(x_, i, s, k):
                act.wait_ge(x_.rows_in[s], (i + 1) * 16 * TJ)
                two = x_.bufs == 2
                act.wait_ge(x_.summed, k + x_.slots - 1 if two else k + 1)
                for j in range(TJ):
                    nc.scalar.activation(hi_b[:, (s % x_.bufs) * TJ + j, :], rows[s][:, j * D:(j + 1) * D], ACT.Copy
                                         ).then_inc(x_.hi, 1)

            def b_stage(x_, s2, k, w):
                act.wait_ge(x_.summed, k + 1 + x_.slots)
                act.wait_ge(x_.stage_free, w + 1)
                nc.scalar.activation(stage_b[:, s2, :], flat[:, 2 * s2 * D:2 * s2 * D + AW], ACT.Copy
                                     ).then_inc(x_.staged, 1)

            def b_round(i, last=False):
                for s in range(B_SLOTS):
                    k = i * B_SLOTS + s
                    if s == 1:
                        act.wait_ge(b_kept, i + 1)
                        nc.scalar.activation(hT_b[:, 0, :], big[:, bass.ds(i * D, D)], ACT.Copy).then_inc(b_hT, 1)
                    if s < B_SLOTS - 1:
                        b_hi(bm, i, s + 1, k + 1)
                    elif not last:
                        b_hi(bm, i + 1, 0, k + 1)
                    if s % 2 == 1:
                        b_stage(bm, s // 2, k, i * 2 + s // 2)

            b_hi(bm, 0, 0, 0)
            with act.Fori(0, NT - 1) as i:
                b_round(i)
            b_round(NT - 1, last=True)
            barrier(act, 2)

            def general_b(x_, g, w, k):
                b_hi(x_, k, 0, k)
                b_stage(x_, 0, k, k)
            general_pass(act, bx, general_b)
            barrier(act, 3)

            def c_step(n, s, r):
                if has(n, 2):
                    act.wait_ge(c_var2, n - 1)
                    nc.scalar.activation(std2[:, s, :], mean_var2[:, s, 1:2], ACT.Sqrt, bias=eps_t[:, :]
                                         ).then_inc(c_std2, 1)
                if has(n):
                    act.wait_ge(c_var, n + 1)
                    nc.scalar.activation(std[:, s, :], mean_var[:, s, 1:2], ACT.Sqrt, bias=eps_t[:, :]
                                         ).then_inc(c_std, 1)
                if has(n, 2):
                    act.wait_ge(c_shift2, n - 1)
                    nc.scalar.activation(h2_t[:, s, :], x2_t[:, s, :], ACT.Relu, bias=shift2[:, s, :],
                                         scale=rstd2[:, s, :]).then_inc(c_h2, 1)
                if has(n):
                    act.wait_ge(c_shift, n + 1)
                    nc.scalar.activation(y_t[:, s, :], h0_t[:, s, :], ACT.Identity, bias=shift[:, s, :],
                                         scale=rstd[:, s, :]).then_inc(c_y, 1)
                if has(n, 2):
                    act.wait_ge(c_T, n - 1)
                    nc.scalar.activation(h2T_t[:, s, :], psum[:, s, :], ACT.Copy).then_inc(c_Tc, 1)
                if has(n, 3):
                    act.wait_ge(c_up, n - 2)
                    if has(n, 3, least=5):
                        act.wait_ge(c_up_out[1 - s], (r - 2 + s) * 16)
                    nc.scalar.activation(up_t[:, 1 - s, :], psum[:, 3 - s, :], ACT.Copy).then_inc(c_upc, 1)

            rounds(act, c_step, NT + 3)
            barrier(act, 4)

            act.sem_inc(dm.act[2], 1)
            act.sem_inc(dx.act[2], 1)
            act.sem_inc(dm.sum_copied, 1)
            act.sem_inc(dx.sum_copied, 1)
            act.sem_inc(dm.T_copied, 1)
            act.sem_inc(dx.T_copied, 1)
            act.sem_inc(dm.staged, dm.bufs)
            act.sem_inc(dx.staged, dx.bufs)
            scales = [BASIS ** -0.5, SILU_2MOM * HID ** -0.5, SILU_2MOM * HID ** -0.5]

            def silu(x_, n, k, s):
                act.wait_ge(x_.layer[n], k + 1)
                to = (h1[:, 0, :], h2[:, 0, :], h3[:, s, :])[n]
                nc.scalar.activation(to, psum[:, 0, 0:HALF], ACT.Silu, scale=scales[n]).then_inc(x_.act[n], 1)

            def copy_sum(x_, k, w):
                act.wait_ge(x_.tile, k * TJ + TJ + RING)
                act.wait_ge(x_.T, w + 1)
                nc.scalar.activation(sum_sb[:, 0, :], flat[:, 3 * D:5 * D], ACT.Copy).then_inc(x_.sum_copied, 1)

            def copy_T(x_, w):
                act.wait_ge(x_.T, w + 2)
                act.wait_ge(x_.o, w + 1)
                nc.scalar.activation(sumT_sb[:, 0, :], flat[:, 5 * D:7 * D], ACT.Copy).then_inc(x_.T_copied, 1)

            def copy_o(x_, w, s):
                act.wait_ge(x_.o, w + 2)
                act.wait_ge(x_.stage_free, w + 1)
                nc.scalar.activation(o_sb[:, s, 0:MUL], psum[:, 7, 0:MUL], ACT.Copy)
                nc.scalar.activation(o_sb[:, s, MUL:4 * MUL].rearrange("p (v m) -> p m v", m=3),
                                     psum[:, 7, MUL:4 * MUL].rearrange("p (m v) -> p m v", m=3),
                                     ACT.Copy).then_inc(x_.staged, 1)

            def parts(x_, g, k, j):
                T, b = k * TJ + j, j
                act.wait_ge(x_.prod, T + 1 + TJ * x_.slots)
                y = [attr[:, 0, bass.ds((g * TJ + j) * 4 + c, 1)] for c in range(4)]
                for c in range(3):
                    nc.scalar.activation(prod[:, b, (5 + c) * MUL:(6 + c) * MUL], u_of(b), ACT.Copy, scale=y[1 + c]
                                         ).then_inc(x_.p2, 1)
                act.wait_ge(x_.tile, T + 1)
                nc.scalar.activation(hi[:, b, 0:D], prod[:, b, 0:D], ACT.Copy, scale=y[0])
                act.wait_ge(x_.p2, T * 3 + 3)
                nc.scalar.activation(hi[:, b, D:], prod[:, b, D:], ACT.Copy).then_inc(x_.hi, 1)

            def d_step(k, s, i, known=None):
                def has(step):
                    return known is None or 0 <= known + step < NG
                if has(0):
                    parts(dm, k, k, 0)
                if has(1):
                    silu(dm, 2, k + 1, 1 - s % 2)
                if has(0):
                    parts(dm, k, k, 1)
                if s % 2 == 0 and has(-1):
                    copy_sum(dm, k - 1, i * 2 + s // 2 - 1)
                if s % 2 == 1 and has(-2):
                    copy_T(dm, i * 2 + s // 2 - 1)
                if has(0):
                    parts(dm, k, k, 2)
                if has(2):
                    silu(dm, 0, k + 2, s % 2)
                if s % 2 == 1 and has(-4):
                    copy_o(dm, i * 2 + s // 2 - 2, s // 2 % 2)
                if has(0):
                    parts(dm, k, k, 3)
                if has(2):
                    silu(dm, 1, k + 2, s % 2)

            for n in range(3):
                silu(dm, n, 0, 0)
            for n in range(2):
                silu(dm, n, 1, 1)
            for k in range(D_SLOTS):
                d_step(k, k, 0, known=k)
            with act.Fori(1, NG // D_SLOTS - 1) as i:
                for s in range(D_SLOTS):
                    d_step(i * D_SLOTS + s, s, i)
            for k in range(NG - D_SLOTS, NG + 4):
                d_step(k, k % D_SLOTS, k // D_SLOTS, known=k)
            barrier(act, 5)

            def general_d(x_, g, w, k):
                for n in range(3):
                    silu(x_, n, k, 0)
                for j in range(TJ):
                    parts(x_, g, k, j)
                copy_sum(x_, k, k)
                copy_T(x_, k)
                copy_o(x_, k, 0)
            general_pass(act, dx, general_d)

        @block.vector
        def _(dve):
            setup = Chain(dve, s_setup)
            nc.vector.memset(zero, 0.0).then_inc(s_zeroed, 1)
            dve.wait_ge(s_dst, 16)
            rows2 = dst_r_i[:, :].rearrange("p (c e) -> p c e", c=2)
            setup.link(nc.vector.tensor_reduce(least_g[:, :], rows2, AX.X, ALU.min))
            setup.link(nc.vector.tensor_reduce(more[:, :], rows2, AX.X, ALU.max))
            setup.link(nc.vector.tensor_tensor(least[:, :], least_g[:, 0:1].to_broadcast([GP, 2]),
                                               least_g[:, 1:2].to_broadcast([GP, 2]), ALU.min))
            setup.link(nc.vector.tensor_tensor(more[:, :], more[:, :], least[:, :], ALU.subtract))
            nc.vector.tensor_scalar(more[:, :], more[:, :], int(math.log2(P)), None, ALU.arith_shift_right
                                    ).then_inc(s_meta_made, 1)

            def a_step(n, s, r):
                if has(n):
                    chain = Chain(dve, a_chain, n * 2)
                    dve.wait_ge(a_x_in[s], (r + 1) * 16)
                    chain.link(nc.vector.bn_stats(stats[:, s, :], xt[:, s, :]))
                    hold(dve)
                    nc.vector.bn_aggr(mean_var[:, s, :], stats[:, s, :]).then_inc(a_var, 1)
                    dve.wait_ge(a_std, n + 1)
                    chain.link(nc.vector.reciprocal(rstd[:, s, :], std[:, s, :]))
                    nc.vector.tensor_scalar(shift[:, s, :], mean_var[:, s, 0:1], rstd[:, s, :], -1.0,
                                            ALU.mult, ALU.mult).then_inc(a_shift, 1)
                if has(n, 1):
                    dve.wait_ge(a_Tc, n)
                    nc.vector.tensor_copy(big[:, bass.ds((n - 1) * D, D)], h_t[:, 1 - s, :]).then_inc(a_kept, 1)
                if has(n):
                    dve.wait_ge(a_h, n + 1)
                    if has(n, 2):
                        dve.wait_ge(a_res_out[s], r * 16)
                    nc.vector.tensor_tensor(res_t[:, s, :], xt[:, s, :], ht[:, s, :], ALU.add).then_inc(a_res, 1)

            rounds(dve, a_step, NT + 1)

            dve.wait_ge(s_dst_cols, 16)
            dve.wait_ge(s_meta_in, 32)
            setup.link(nc.vector.memset(zero_f[:, :], 0.0))
            setup.link(nc.vector.tensor_copy(more_f[:, :], meta_row[0:1, MORE:MORE + NG]))
            setup.link(nc.vector.tensor_tensor_scan(prefix_f[:, :], more_f[:, :], zero_f[:, :], 0.0,
                                                    ALU.add, ALU.add))
            setup.link(nc.vector.tensor_copy(meta_row[0:1, TOTAL:TOTAL + 1], prefix_f[0:1, NG - 1:NG]))
            setup.link(nc.vector.tensor_tensor(meta_row[0:1, BEFORE:BEFORE + NG], prefix_f[:, :], more_f[:, :],
                                               ALU.subtract))
            setup.link(nc.vector.tensor_scalar(more_f[:, :], more_f[:, :], 1.0, None, ALU.min))
            for n, v in enumerate((from_end, from_start)):
                setup.link(nc.vector.tensor_tensor(v[:, :], v[:, :], more_f[:, :], ALU.mult))
                setup.link(nc.vector.tensor_reduce(bound_f[:, n:n + 1], v[:, :], AX.X, ALU.max))
            setup.link(nc.vector.tensor_scalar(meta_row[0:1, FIRST:FIRST + 1], bound_f[:, 0:1], -1.0, float(NG),
                                               ALU.mult, ALU.add))
            setup.link(nc.vector.tensor_scalar(meta_row[0:1, SPAN:SPAN + 1], bound_f[:, 1:2], bound_f[:, 0:1],
                                               -float(NG), ALU.add, ALU.add))
            start_v = start_bc[:, :].unsqueeze(2).to_broadcast([P, NG, TJ])
            setup.link(nc.vector.tensor_tensor(rel[:, :].rearrange("p (g j) -> p g j", j=TJ),
                                               dst_c_i[:, :].rearrange("p (g j) -> p g j", j=TJ), start_v,
                                               ALU.subtract))
            full, part = divmod(N_EDGES, P)
            for p0 in range(part, P, 32):
                setup.link(nc.vector.memset(rel[p0:p0 + 32, full:full + 1], DEAD))
            setup.link(nc.vector.memset(rel[:, full + 1:], DEAD))
            dve.wait_ge(s_w, 7 * 16)
            nc.vector.tensor_scalar(w_up[:, :, :], w_up[:, :, :], MUL ** -0.5, None, ALU.mult)
            barrier(dve, 1)

            def select(x_, rel_of, s):
                nc.vector.tensor_tensor(sel[:, s, :].rearrange("p (j n) -> p j n", j=TJ),
                                        iota_n[:, :].unsqueeze(1).to_broadcast([P, TJ, P]),
                                        rel_of.unsqueeze(2).to_broadcast([P, TJ, P]), ALU.is_equal
                                        ).then_inc(x_.sel, 1)

            def rel_main(g):
                return rel[:, bass.ds(g * TJ, TJ)]

            def rel_of_window(x_, g, w, k):
                nc.vector.tensor_scalar(rel_w[:, :], rel[:, bass.ds(g * TJ, TJ)], window_start[:, bass.ds(w, 1)],
                                        None, ALU.subtract).then_inc(x_.relw, 1)
                dve.wait_ge(x_.relw, k + 1)
                return rel_w[:, :]

            def b_lo(x_, s, k):
                for j in range(TJ):
                    dve.wait_ge(x_.hi, (k + x_.slots) * TJ + j + 1)
                    b = (s % x_.bufs) * TJ + j
                    nc.vector.tensor_tensor(lo_b[:, b, :], rows[s][:, j * D:(j + 1) * D],
                                            hi_b[:, b, :].bitcast(F32), ALU.subtract).then_inc(x_.lo, 1)

            dve.sem_inc(b_kept, 1)
            dve.sem_inc(bm.lo, TJ * bm.slots)
            dve.sem_inc(bx.lo, TJ * bx.slots)
            with dve.Fori(0, NT) as i:
                for s in range(B_SLOTS):
                    k = i * B_SLOTS + s
                    dve.wait_ge(bm.summed, k + 1)
                    select(bm, rel_main(k), s)
                    b_lo(bm, s, k)
                    if s == 2:
                        dve.wait_ge(b_self_mm, i + 1)
                        nc.vector.tensor_tensor(self_part[:, bass.ds(i * D, D)], psum[:, 4, :], bias_bc[:, :],
                                                ALU.add).then_inc(b_kept, 1)
            barrier(dve, 2)

            def general_b(x_, g, w, k):
                dve.wait_ge(x_.summed, k + 1)
                select(x_, rel_of_window(x_, g, w, k), 0)
                b_lo(x_, 0, k)
            general_pass(dve, bx, general_b)
            barrier(dve, 3)

            def c_step(n, s, r):
                here, behind = has(n), has(n, 2)
                m = n - 2
                y = y_t[:, s, :]
                if behind:
                    dve.wait_ge(c_affine, m * 2 + 2)
                    nc.vector.tensor_scalar(neg_t[:, 0, :], y, 0.0, alpha_bc[:, :], ALU.min, ALU.mult
                                            ).then_inc(c_chain_out, 1)
                if here:
                    dve.wait_ge(c_acc_in[s], (r + 1) * 16)
                    nc.vector.tensor_scalar(deg[:, s, :], acc_t[:, s, D:AW], 1.0, None, ALU.max
                                            ).then_inc(c_chain_in, 1)
                if behind:
                    dve.wait_ge(c_chain_out, m * 4 + 1)
                    nc.vector.scalar_tensor_tensor(y, y, 0.0, neg_t[:, 0, :], ALU.max, ALU.add
                                                   ).then_inc(c_chain_out, 1)
                if here:
                    dve.wait_ge(c_chain_in, n * 5 + 1)
                    nc.vector.reciprocal(rdeg[:, s, :], deg[:, s, :]).then_inc(c_chain_in, 1)
                if behind:
                    dve.wait_ge(c_res_in[s], r * 16)
                    if has(n, 2, least=4):
                        dve.wait_ge(c_x2_out[s], (r - 1) * 16)
                        dve.wait_ge(c_h2, n - 3)
                    dve.wait_ge(c_chain_out, m * 4 + 2)
                    nc.vector.tensor_tensor(x2_t[:, s, :], y, res_c[:, s, :], ALU.add).then_inc(c_x2, 1)
                if here:
                    dve.wait_ge(c_chain_in, n * 5 + 2)
                    nc.vector.scalar_tensor_tensor(
                        h0_t[:, s, :], acc_t[:, s, 0:D], rdeg[:, s, :], self_part[:, bass.ds(n * D, D)],
                        ALU.mult, ALU.add).then_inc(c_chain_in, 1)
                if behind:
                    dve.wait_ge(c_x2, m + 1)
                    nc.vector.bn_stats(stats2[:, s, :], x2_t[:, s, :]).then_inc(c_chain_out, 1)
                if here:
                    dve.wait_ge(c_chain_in, n * 5 + 3)
                    nc.vector.bn_stats(stats[:, s, :], h0_t[:, s, :]).then_inc(c_chain_in, 1)
                if behind:
                    dve.wait_ge(c_chain_out, m * 4 + 3)
                    hold(dve)
                    nc.vector.bn_aggr(mean_var2[:, s, :], stats2[:, s, :]).then_inc(c_var2, 1)
                if here:
                    dve.wait_ge(c_chain_in, n * 5 + 4)
                    hold(dve)
                    nc.vector.bn_aggr(mean_var[:, s, :], stats[:, s, :]).then_inc(c_var, 1)
                if behind:
                    dve.wait_ge(c_std2, m + 1)
                    nc.vector.reciprocal(rstd2[:, s, :], std2[:, s, :]).then_inc(c_chain_out, 1)
                if here:
                    dve.wait_ge(c_std, n + 1)
                    nc.vector.reciprocal(rstd[:, s, :], std[:, s, :]).then_inc(c_chain_in, 1)
                if behind:
                    dve.wait_ge(c_chain_out, m * 4 + 4)
                    nc.vector.tensor_scalar(shift2[:, s, :], mean_var2[:, s, 0:1], rstd2[:, s, :], -1.0,
                                            ALU.mult, ALU.mult).then_inc(c_shift2, 1)
                if here:
                    dve.wait_ge(c_chain_in, n * 5 + 5)
                    nc.vector.tensor_scalar(shift[:, s, :], mean_var[:, s, 0:1], rstd[:, s, :], -1.0,
                                            ALU.mult, ALU.mult).then_inc(c_shift, 1)

            rounds(dve, c_step, NT + 2)
            barrier(dve, 4)

            dve.wait_ge(s_dw, 6 * 16)
            silu_scale = SILU_2MOM * HID ** -0.5
            nc.vector.tensor_scalar(w4_sb[:, 0, 0:3 * MUL], w4_sb[:, 0, 0:3 * MUL], silu_scale, None, ALU.mult)
            nc.vector.tensor_scalar(w4_sb[:, 0, 3 * MUL:], w4_sb[:, 0, 3 * MUL:], silu_scale / math.sqrt(3.0),
                                    None, ALU.mult)
            nc.vector.tensor_scalar(wout_sb[:, :, :], wout_sb[:, :, :], (2 * MUL) ** -0.5 / AVG_NEIGHBORS,
                                    None, ALU.mult).then_inc(s_dw_scaled, 1)
            for x_ in (dm, dx):
                dve.sem_inc(x_.prod, TJ * x_.slots)
                dve.sem_inc(x_.lo_v, RING)
            dve.wait_ge(s_attr, 16)

            def products(x_, g, s, k, j, between=None):
                T, b = k * TJ + j, j
                m, w = prod[:, b, :], psum[:, 1 + j % 2, :]
                row = rows[s][:, j * D:(j + 1) * D]
                s0, s1 = row[:, 0:MUL], row[:, MUL:]
                y = [attr[:, 0, bass.ds((g * TJ + j) * 4 + c, 1)] for c in range(4)]
                q = q_t[:, b, :]
                dve.wait_ge(x_.lo_v, T + 1)
                dve.wait_ge(x_.lo_p, T + 1)
                nc.vector.tensor_scalar(q[:, 0:MUL], s1[:, 0:MUL], y[1], None, ALU.mult).then_inc(x_.q, 1)
                dve.wait_ge(x_.weights, T + 1)
                nc.vector.tensor_tensor(m[:, MUL:D].rearrange("p (m c) -> p m c", m=3),
                                        w[:, 2 * MUL:3 * MUL].unsqueeze(1).to_broadcast([P, 3, MUL]),
                                        s1.rearrange("p (m c) -> p m c", m=3), ALU.mult)
                dve.wait_ge(x_.q, T * 3 + 1)
                nc.vector.scalar_tensor_tensor(q[:, MUL:2 * MUL], s1[:, MUL:2 * MUL], y[2], q[:, 0:MUL],
                                               ALU.mult, ALU.add).then_inc(x_.q, 1)
                if between:
                    lo_tile(*between)
                dve.wait_ge(x_.q, T * 3 + 2)
                nc.vector.scalar_tensor_tensor(q[:, 2 * MUL:], s1[:, 2 * MUL:], y[3], q[:, MUL:2 * MUL],
                                               ALU.mult, ALU.add).then_inc(x_.q, 1)
                nc.vector.tensor_tensor(p1_u(b), w[:, 0:2 * MUL].rearrange("p (a c) -> p a c", a=2),
                                        s0.unsqueeze(1).to_broadcast([P, 2, MUL]), ALU.mult)
                dve.wait_ge(x_.q, T * 3 + 3)
                nc.vector.tensor_tensor(m[:, D:D + MUL], w[:, 3 * MUL:], q[:, 2 * MUL:], ALU.mult
                                        ).then_inc(x_.prod, 1)

            def lo_tile(x_, g, k, j):
                T, b = k * TJ + j, j
                dve.wait_ge(x_.hi, T + 1)
                nc.vector.scalar_tensor_tensor(lo[:, b, 0:D], prod[:, b, 0:D],
                                               attr[:, 0, bass.ds((g * TJ + j) * 4, 1)],
                                               hi[:, b, 0:D].bitcast(F32), ALU.mult, ALU.subtract
                                               ).then_inc(x_.lo_v, 1)

            def d_step(i, s, first=False):
                k = i * D_SLOTS + s
                select(dm, rel_main(k), s)
                dve.wait_ge(dm.rows_in[s], (i + 1) * 16 * TJ)
                for j in range(TJ):
                    between = (dm, k, k, j - 2) if j >= 2 else None if first else (dm, k - 1, k - 1, j + 2)
                    products(dm, k, s, k, j, between)

            for s in range(D_SLOTS):
                d_step(0, s, first=(s == 0))
            with dve.Fori(1, NG // D_SLOTS) as i:
                for s in range(D_SLOTS):
                    d_step(i, s)
            lo_tile(dm, NG - 1, NG - 1, 2)
            lo_tile(dm, NG - 1, NG - 1, 3)
            barrier(dve, 5)

            def general_d(x_, g, w, k):
                rel_of = rel_of_window(x_, g, w, k)
                dve.wait_ge(x_.tile, k * TJ + RING)
                select(x_, rel_of, 0)
                dve.wait_ge(x_.rows_in[0], (k + 1) * 16 * TJ)
                for j in range(TJ):
                    products(x_, g, 0, k, j)
                    lo_tile(x_, g, k, j)
            general_pass(dve, dx, general_d)

        @block.tensor
        def _(pe):
            pe.wait_ge(s_const, 1)
            pe.wait_ge(s_wn, 16)

            def a_step(n, s, r):
                if has(n):
                    pe.wait_ge(a_h, n + 1)
                    for c in range(KC):
                        last = nc.tensor.transpose(psum[:, s, c * P:(c + 1) * P], ht[:, s, c * P:(c + 1) * P],
                                                   ident[:, :])
                    last.then_inc(a_T, 1)
                if has(n, 1):
                    pe.wait_ge(a_Tc, n)
                    if has(n, 1, least=3):
                        pe.wait_ge(a_hn, n - 2)
                    for c in range(KC):
                        last = nc.tensor.matmul(psum[:, 3 - s, :], h_t[:, 1 - s, c * P:(c + 1) * P],
                                                wn_sb[:, c, :], start=(c == 0), stop=(c == KC - 1))
                    last.then_inc(a_mm, 1)

            rounds(pe, a_step, NT + 1)
            barrier(pe, 1)

            pe.sem_inc(bm.summed, bm.slots)
            pe.sem_inc(bx.summed, bx.slots)

            def b_step(x_, s, k, bank, w, parts, first=True, last=True):
                pe.wait_ge(x_.sel, k + 1)
                if first:
                    pe.wait_ge(x_.staged, w + 1)
                for j in range(TJ):
                    sel_j = sel[:, s, j * P:(j + 1) * P]
                    pe.wait_ge(x_.lo, (k + x_.slots) * TJ + j + 1)
                    start, stop = first and j == 0, last and j == TJ - 1
                    for part in (hi_b, lo_b):
                        nc.tensor.matmul(psum[:, 2 * bank, :], sel_j, part[:, parts * TJ + j, :],
                                         start=(start and part is hi_b), stop=(stop and part is lo_b))
                    done = nc.tensor.matmul(psum[:, 2 * bank + 1, 0:2], sel_j, ones[:, :], start=start, stop=stop)
                done.then_inc(x_.summed, 1)

            def self_product(i):
                pe.wait_ge(b_hT, i + 1)
                for c in range(KC):
                    last = nc.tensor.matmul(psum[:, 4, :], hT_b[:, 0, c * P:(c + 1) * P], ws_sb[:, c, :],
                                            start=(c == 0), stop=(c == KC - 1))
                last.then_inc(b_self_mm, 1)

            with pe.Fori(0, NT) as i:
                for s in range(B_SLOTS):
                    b_step(bm, s, i * B_SLOTS + s, s // 2, i * 2 + s // 2, s % 2, first=(s % 2 == 0), last=(s % 2 == 1))
                    if s == 1:
                        self_product(i)
            barrier(pe, 2)
            general_pass(pe, bx, lambda x_, g, w, k: b_step(x_, 0, k, 0, k, 0))
            barrier(pe, 3)

            def c_step(n, s, r):
                pe.wait_ge(c_h2, n + 1)
                h = h2_t[:, s, :]
                nc.tensor.transpose(psum[:, s, 0:P], h[:, 0:MUL], ident[:, :])
                for m in range(3):
                    last = nc.tensor.transpose(psum[:, s, (m + 1) * P:(m + 2) * P], h[:, MUL + m::3], ident[:, :])
                last.then_inc(c_T, 1)
                pe.wait_ge(c_Tc, n + 1)
                if has(n, 2):
                    pe.wait_ge(c_upc, n - 1)
                for m in range(4):
                    last = nc.tensor.matmul(psum[:, 2 + s, m * MUL:(m + 1) * MUL], h2T_t[:, s, m * P:(m + 1) * P],
                                            w_up[:, min(m, 1), :], start=True, stop=True)
                last.then_inc(c_up, 1)

            rounds(pe, c_step, NT)
            barrier(pe, 4)

            pe.wait_ge(s_dw_scaled, 1)
            pe.sem_inc(dm.tile, RING)
            pe.sem_inc(dx.tile, RING)
            pe.sem_inc(dm.T, 1)
            pe.sem_inc(dx.T, 1)
            pe.sem_inc(dm.o, 1)
            pe.sem_inc(dx.o, 1)

            def mlp(x_, n, i, s, k):
                if n == 0:
                    pe.wait_ge(x_.feat_in[s], (i + 1) * 16)
                    pe.wait_ge(x_.act[2], k + 1)
                    w, h = w1_sb[0:2 * BASIS, 0, :], feat_t[0:2 * BASIS, s, :]
                else:
                    pe.wait_ge(x_.act[n - 1], k + 1)
                    w, h = ((w2_sb[:, 0, :], h1[:, 0, :]), (w3_sb[:, 0, :], h2[:, 0, :]))[n - 1]
                nc.tensor.matmul(psum[:, 0, 0:HALF], w, h, start=True, stop=True).then_inc(x_.layer[n], 1)

            def edge_weights(x_, s, k, j):
                T = k * TJ + j
                if j == 0:
                    pe.wait_ge(x_.act[2], k + 2)
                pe.wait_ge(x_.prod, T - 1 + TJ * x_.slots)
                half, col = (j % 2) * HID, (j // 2) * P
                nc.tensor.matmul(psum[:, 1 + j % 2, :], h3[half:half + HID, s % x_.bufs, col:col + P],
                                 w4_sb[half:half + HID, 0, :], start=True, stop=True).then_inc(x_.weights, 1)

            def sum_tile(x_, s, k, j, w, first=True, final=True):
                T = k * TJ + j
                pe.wait_ge(x_.lo_v, T + 1 + RING)
                pe.wait_ge(x_.lo_p, T + 1 + RING)
                if j == 0:
                    pe.wait_ge(x_.sel, k + 1)
                    if first:
                        pe.wait_ge(x_.sum_copied, w + 1)
                for b in range(2):
                    for part in (hi, lo):
                        last = nc.tensor.matmul(psum[:, 3 + b, :], sel[:, s, j * P:(j + 1) * P],
                                                part[:, j, b * D:(b + 1) * D],
                                                start=(first and j == 0 and part is hi),
                                                stop=(final and j == TJ - 1 and part is lo))
                last.then_inc(x_.tile, 1)

            def transpose_sum(x_, w):
                pe.wait_ge(x_.sum_copied, w + 2)
                pe.wait_ge(x_.T_copied, w + 1)
                for c in range(8):
                    last = nc.tensor.transpose(psum[:, 5 + c // 4, (c % 4) * P:(c % 4 + 1) * P],
                                               sum_sb[:, 0, c * P:(c + 1) * P], ident[:, :])
                last.then_inc(x_.T, 1)

            def output_maps(x_, w):
                pe.wait_ge(x_.T_copied, w + 2)
                pe.wait_ge(x_.staged, w + x_.bufs)
                for m in range(4):
                    for c in range(2):
                        at = ((0, 4), (5, 1), (6, 2), (7, 3))[m][c]
                        last = nc.tensor.matmul(psum[:, 7, m * MUL:(m + 1) * MUL],
                                                sumT_sb[:, 0, at * P:(at + 1) * P],
                                                wout_sb[:, 2 * min(m, 1) + c, :], start=(c == 0), stop=(c == 1))
                last.then_inc(x_.o, 1)

            def d_step(i, s, known=None, last=False):
                k = i * D_SLOTS + s

                def has(step):
                    return known is None or 0 <= known + step < NG
                i1, s1 = (i, s + 1) if s + 1 < D_SLOTS else (i + 1, 0)
                for j in range(TJ):
                    if has(0):
                        edge_weights(dm, s, k, j)
                    if j < 3 and not last and has(1):
                        mlp(dm, j, i1, s1, k + 1)
                    if s % 2 == 1 and j == 0 and has(-2):
                        transpose_sum(dm, i * 2 + s // 2 - 1)
                    if has(-1):
                        sum_tile(dm, (s - 1) % D_SLOTS, k - 1, j, i * 2 + (s - 1) // 2,
                                 first=(s % 2 == 1), final=(s % 2 == 0))
                    if s % 2 == 0 and j == 3 and has(-3):
                        output_maps(dm, i * 2 + s // 2 - 2)

            for n in range(3):
                mlp(dm, n, 0, 0, 0)
            for s in range(D_SLOTS):
                d_step(0, s, known=s)
            with pe.Fori(1, NG // D_SLOTS - 1) as i:
                for s in range(D_SLOTS):
                    d_step(i, s)
            for s in range(D_SLOTS):
                d_step(NG // D_SLOTS - 1, s, last=(s == D_SLOTS - 1))
            for s in range(3):
                d_step(NG // D_SLOTS, s, known=NG + s)
            barrier(pe, 5)

            def general_d(x_, g, w, k):
                for n in range(3):
                    mlp(x_, n, k, 0, k)
                for j in range(TJ + 1):
                    if j < TJ:
                        edge_weights(x_, 0, k, j)
                    if j > 0:
                        sum_tile(x_, 0, k, j - 1, k)
                transpose_sum(x_, k)
                output_maps(x_, k)
            general_pass(pe, dx, general_d)


def kernel(x, src, dst, edge_attr_4, edge_attr_8, L0_gnn_W_self, L0_gnn_b_self, L0_gnn_W_neigh, L0_gnn_gamma,
           L0_gnn_beta, L0_gnn_alpha, L1_gnn_W_up0, L1_gnn_W_up1, L1_gnn_W_mlp1, L1_gnn_W_mlp2, L1_gnn_W_mlp3,
           L1_gnn_W_mlp4, L1_gnn_W_out0, L1_gnn_W_out1):
    import concourse.bacc as bacc
    from concourse.bass_utils import run_bass_kernel_spmd

    a = np.asarray
    n_pad = NG * GE - N_EDGES

    def edge_pad(v):
        return np.concatenate([a(v), np.repeat(a(v)[-1:], n_pad, axis=0)])

    def to_rows(v):
        return np.ascontiguousarray(np.broadcast_to(a(v).reshape(1, -1), (P, a(v).size)))

    def columns(v):
        return np.ascontiguousarray(v.reshape(NG, TJ, P, -1).transpose(2, 0, 1, 3).reshape(P, -1))

    def block_diagonal(w):
        w = a(w)
        both = np.zeros((2 * w.shape[0], 2 * w.shape[1]), w.dtype)
        both[:w.shape[0], :w.shape[1]] = w
        both[w.shape[0]:, w.shape[1]:] = w
        return both

    x_pad = np.zeros((NP, D), a(x).dtype)
    x_pad[:N_NODES] = a(x)
    src_p, dst_p = edge_pad(src), edge_pad(dst)
    ins = {
        "x": x_pad,
        "src_g": np.ascontiguousarray(src_p.reshape(NG, TJ, P).transpose(0, 2, 1)),
        "dst_rows": dst_p.reshape(GP, 2 * GE),
        "dst_cols": columns(dst_p),
        "attr_cols": columns(edge_pad(edge_attr_4)),
        "feat_g": np.ascontiguousarray(edge_pad(edge_attr_8).reshape(NG, 2, 2, P, BASIS).transpose(0, 2, 4, 1, 3)
                                       .reshape(NG, 2 * BASIS, HALF)),
        "w_self": a(L0_gnn_W_self), "w_neigh": a(L0_gnn_W_neigh),
        "b_self": to_rows(L0_gnn_b_self), "gamma": to_rows(L0_gnn_gamma), "beta": to_rows(L0_gnn_beta),
        "alpha": to_rows(L0_gnn_alpha),
        "w_up0": a(L1_gnn_W_up0), "w_up1": a(L1_gnn_W_up1),
        "w_mlp1": block_diagonal(L1_gnn_W_mlp1), "w_mlp2": block_diagonal(L1_gnn_W_mlp2),
        "w_mlp3": block_diagonal(L1_gnn_W_mlp3),
        "w_mlp4": np.concatenate([a(L1_gnn_W_mlp4)] * 2),
        "w_out0": a(L1_gnn_W_out0), "w_out1": a(L1_gnn_W_out1),
    }
    nc = bacc.Bacc("TRN2", target_bir_lowering=False, num_devices=1)
    aps = {name: nc.dram_tensor(f"in_{name}", v.shape, mybir.dt.from_np(v.dtype), kind="ExternalInput").ap()
           for name, v in ins.items()}
    out = nc.dram_tensor("out_0", (WINDOW_ROWS, D), F32, kind="ExternalOutput").ap()
    gnn_kernel(nc, *aps.values(), out)
    r = run_bass_kernel_spmd(nc, [{f"in_{name}": v for name, v in ins.items()}], core_ids=[0])
    return r.results[0]["out_0"][:N_NODES]
```
